# Optimizing a Trainium2 kernel written in Bass

```python
import numpy as np
import jax
import jax.numpy as jnp

def _softmax(x, axis=-1):
    return jax.nn.softmax(x, axis=axis)

def _gelu(x):
    return jax.nn.gelu(x, approximate=True)

def _silu(x):
    return jax.nn.silu(x)

def _sigmoid(x):
    return jax.nn.sigmoid(x)

def _layernorm(x, axis=-1, eps=1e-05):
    m = jnp.mean(x, axis=axis, keepdims=True)
    v = jnp.var(x, axis=axis, keepdims=True)
    return (x - m) / jnp.sqrt(v + eps)

def _scatter_add(tgt, idx, src, axis=0):
    return tgt.at[idx].add(src)

def _segment_sum(src, seg, n):
    return jax.ops.segment_sum(src, seg, n)
kernel_name = 'mk_gnn_ffn_d1_gnn_r8_0303ff'

def setup_inputs(seed: int=0):
    np.random.seed(seed)
    _w = jnp.asarray

    def _rec_inputs():
        import jax
        import jax.numpy as jnp
        _gk = jax.random.key(seed)
        x = -7.329e-05 + 0.9999 * jax.random.normal(jax.random.fold_in(_gk, 1), (6250, 256), jnp.float32)
        _s = jax.random.randint(jax.random.fold_in(_gk, 2), (50000,), 0, 6250, jnp.int32)
        _d = jax.random.randint(jax.random.fold_in(_gk, 3), (50000,), 0, 6250, jnp.int32)
        _loop = jnp.arange(6250, dtype=jnp.int32)
        src = jnp.concatenate([_s, _d, _loop])
        dst = jnp.concatenate([_d, _s, _loop])
        _o = jnp.argsort(dst, stable=True)
        src = src[_o]
        dst = dst[_o]
        return (x, src, dst)
    x, src, dst = _rec_inputs()

    def _L0_gnn_setup():
        import jax, jax.numpy as jnp
        import numpy as np
        V = 25000
        E = 75000
        INPUT_DIM = 256
        OUTPUT_DIM = 256
        SUPPORT_DIM = 128
        key = jax.random.key(seed)
        k1, k2, k3 = jax.random.split(key, 3)
        verts = jax.random.normal(k1, (V, INPUT_DIM), dtype=jnp.float32)
        edges = jax.random.randint(k2, (E, 2), 0, V, dtype=jnp.int64)
        kw0, kw1 = jax.random.split(k3)
        w0_w = jax.random.normal(kw0, (OUTPUT_DIM, INPUT_DIM), dtype=jnp.float32) * 0.01
        w0_b = jnp.zeros((OUTPUT_DIM,), dtype=jnp.float32)
        w1_w = jax.random.normal(kw1, (SUPPORT_DIM, INPUT_DIM), dtype=jnp.float32) * 0.01
        w1_b = jnp.zeros((SUPPORT_DIM,), dtype=jnp.float32)
        return {'verts': verts, 'edges': edges, 'w0_w': w0_w, 'w0_b': w0_b, 'w1_w': w1_w, 'w1_b': w1_b}
    _L0_gnn_all = _L0_gnn_setup()
    _L0_gnn_in = {k: v for k, v in _L0_gnn_all.items() if k in ('w0_w', 'w0_b', 'w1_w', 'w1_b')}
    del _L0_gnn_all

    def _L0_ffn_setup():
        import jax, jax.numpy as jnp
        import numpy as np
        C = 256
        HID = 1024
        E = 8
        TEMP = 1.0
        key = jax.random.key(seed)
        ks = jax.random.split(key, 7)
        x = jax.random.normal(ks[0], (8, 2048, C), dtype=jnp.float32)
        W1 = jax.random.normal(ks[1], (C, HID), dtype=jnp.float32) * 0.02
        b1 = jnp.zeros((HID,), dtype=jnp.float32)
        Wg = jax.random.normal(ks[2], (HID, E), dtype=jnp.float32) * 0.02
        bg = jnp.zeros((E,), dtype=jnp.float32)
        Wd = jax.random.normal(ks[3], (E, HID, C), dtype=jnp.float32) * 0.02
        bd = jnp.zeros((E, C), dtype=jnp.float32)
        return {'x': x, 'W1': W1, 'b1': b1, 'Wg': Wg, 'bg': bg, 'Wd': Wd, 'bd': bd}
    _L0_ffn_all = _L0_ffn_setup()
    _L0_ffn_in = {k: v for k, v in _L0_ffn_all.items() if k in ('W1', 'b1', 'Wg', 'bg', 'Wd', 'bd')}
    del _L0_ffn_all
    return {'x': x, 'src': src, 'dst': dst, 'L0_gnn_w0_w': _L0_gnn_in['w0_w'], 'L0_gnn_w0_b': _L0_gnn_in['w0_b'], 'L0_gnn_w1_w': _L0_gnn_in['w1_w'], 'L0_gnn_w1_b': _L0_gnn_in['w1_b'], 'L0_ffn_W1': _L0_ffn_in['W1'], 'L0_ffn_b1': _L0_ffn_in['b1'], 'L0_ffn_Wg': _L0_ffn_in['Wg'], 'L0_ffn_bg': _L0_ffn_in['bg'], 'L0_ffn_Wd': _L0_ffn_in['Wd'], 'L0_ffn_bd': _L0_ffn_in['bd']}

def reference(x, src, dst, L0_gnn_w0_w, L0_gnn_w0_b, L0_gnn_w1_w, L0_gnn_w1_b, L0_ffn_W1, L0_ffn_b1, L0_ffn_Wg, L0_ffn_bg, L0_ffn_Wd, L0_ffn_bd):
    import jax
    import jax.numpy as jnp

    def _L0_gnn_ref(verts, edges, w0_w, w0_b, w1_w, w1_b):
        import jax, jax.numpy as jnp
        import numpy as np
        V = 25000
        E = 75000
        INPUT_DIM = 256
        OUTPUT_DIM = 256
        SUPPORT_DIM = 128
        verts_w0 = verts @ w0_w.T + w0_b
        verts_w1 = verts @ w1_w.T + w1_b
        src = jnp.concatenate([edges[:, 1], edges[:, 0]])
        dst = jnp.concatenate([edges[:, 0], edges[:, 1]])
        neighbor_sums = jax.ops.segment_sum(verts_w1[src], dst, num_segments=verts.shape[0])
        pad = verts_w0.shape[1] - neighbor_sums.shape[1]
        out = verts_w0 + jnp.pad(neighbor_sums, ((0, 0), (0, pad)))
        return out

    def _L0_ffn_ref(x, W1, b1, Wg, bg, Wd, bd):
        import jax, jax.numpy as jnp
        import numpy as np
        C = 256
        HID = 1024
        E = 8
        TEMP = 1.0
        orig_shape = x.shape
        xf = x.reshape(-1, orig_shape[-1])
        H = jax.nn.gelu(xf @ W1 + b1, approximate=False)
        probs = jax.nn.softmax((H @ Wg + bg) / TEMP, axis=-1)
        assign = jnp.argmax(probs, axis=-1)
        out = jnp.zeros_like(xf)
        for e in range(Wd.shape[0]):
            y = H @ Wd[e] + bd[e]
            sel = (assign == e)[:, None]
            out = out + jnp.where(sel, probs[:, e:e + 1] * y, 0.0)
        return out.reshape(orig_shape)
    edge_index_t = jnp.stack([src, dst], axis=1)
    x = x + _L0_gnn_ref(_layernorm(x, axis=-1), edge_index_t, L0_gnn_w0_w, L0_gnn_w0_b, L0_gnn_w1_w, L0_gnn_w1_b)
    x = x + _L0_ffn_ref(_layernorm(x, axis=-1)[None], L0_ffn_W1, L0_ffn_b1, L0_ffn_Wg, L0_ffn_bg, L0_ffn_Wd, L0_ffn_bd)[0]
    return x

_drawn_inputs = setup_inputs


def setup_inputs(seed=0):
    import zlib

    import numpy as np

    out = dict(_drawn_inputs(seed))
    spreads = {'L0_gnn_w0_b': (0.0, 0.1),
     'L0_gnn_w1_b': (0.0, 0.1),
     'L0_ffn_b1': (0.0, 0.8),
     'L0_ffn_bg': (0.0, 0.8),
     'L0_ffn_bd': (0.0, 0.8)}
    factors = {'L0_ffn_W1': 8.0, 'L0_ffn_Wg': 8.0, 'L0_ffn_Wd': 8.0}
    for name, (base, spread) in spreads.items():
        noise = np.random.default_rng([zlib.crc32(name.encode()), seed]).standard_normal(out[name].shape)
        drawn = base * np.exp(spread * noise) if base else spread * noise
        out[name] = jnp.asarray(drawn.astype(out[name].dtype))
    for name, factor in factors.items():
        out[name] = (out[name] * factor).astype(out[name].dtype)
    return out
```

```python
import concourse.bass as bass
from concourse import mybir
from contextlib import ExitStack

P = 128
D = 256
DN = 128
HID = 1024
EXPERTS = 8
NODES = 6250
EDGES = 106250
EPS = 1e-5

TILES = 52
GT = 4
GROUPS = TILES // GT
GN = GT * P
SRC_TILES = 49
SRC_PAD = 50
WIN = 16
WPG = GN // WIN
WINDOWS = GROUPS * WPG
WCOL = SRC_PAD * WIN
HALF = WCOL // 2
CHUNKS = -(-EDGES // P)
CHUNK_TILES = -(-CHUNKS // P)
CHUNKS_PAD = CHUNK_TILES * P
WIN_TILES = -(-WINDOWS // P)
WIN_PAD = WIN_TILES * P
NO_NODE = 8192
SUB = 16
RING = 4
PARTS = 3
PAIRS = (SRC_TILES - 1) // GT // 2
BLOCKS = 2 * PAIRS + 1
RESULTS = BLOCKS + 1


class Steps:

    def __init__(self, eng, sem):
        self.eng, self.sem, self.base, self.n = eng, sem, 0, 0

    def at(self, base):
        self.base, self.n = base, 0

    def done(self, ins):
        ins.then_inc(self.sem, 1)
        self.n += 1
        return ins

    def wait(self):
        self.eng.wait_ge(self.sem, self.base + self.n)


def build(nc, x, src_cols, dst_cols, dst_chunks, w01, b01, W1, b1, Wg, bg, Wd, bd, out):
    f32, f16, bf16, i32 = (mybir.dt.float32, mybir.dt.float16, mybir.dt.bfloat16, mybir.dt.int32)
    ALU, ACT, AX = mybir.AluOpType, mybir.ActivationFunctionType, mybir.AxisListType
    ds = bass.ds

    with ExitStack() as whole:
        def allocators(ctx):
            return (lambda n, s, d: ctx.enter_context(nc.sbuf_tensor(n, s, d)),
                    lambda n, s, d: ctx.enter_context(nc.psum_tensor(n, s, d)),
                    lambda n: ctx.enter_context(nc.semaphore(n)))

        sb, _, sem = allocators(whole)
        residual = nc.dram_tensor("residual", [TILES * P, D], f32, kind="Internal").ap()
        span_lo = nc.dram_tensor("span_lo", [WIN_PAD], f32, kind="Internal").ap()
        span_hi = nc.dram_tensor("span_hi", [WIN_PAD], f32, kind="Internal").ap()
        chunk_min = nc.dram_tensor("chunk_min", [CHUNKS_PAD], f32, kind="Internal").ap()
        chunk_max = nc.dram_tensor("chunk_max", [CHUNKS_PAD], f32, kind="Internal").ap()
        sumT = sb("sumT", [P, TILES * P], f32)
        ident_f = sb("ident_f", [P, P], f32)
        ident_h = sb("ident_h", [P, P], f16)

        with ExitStack() as front:
            sbf, _, _ = allocators(front)
            v1p = sbf("v1p", [P, PARTS, TILES, DN], bf16)
            prepare(nc, allocators, x, w01, b01, residual, v1p, ident_f, ident_h,
                    f32, f16, bf16, i32, ALU, ACT, AX, ds)
            graph(nc, allocators, src_cols, dst_cols, dst_chunks, span_lo, span_hi, chunk_min, chunk_max, v1p, sumT, ident_h,
                  f32, f16, bf16, i32, ALU, ACT, AX, ds)
        ffn(nc, allocators, residual, sumT, ident_f, W1, b1, Wg, bg, Wd, bd, out,
            f32, f16, bf16, i32, ALU, ACT, AX, ds)


def flat2(ap):
    return ap.rearrange("p a d -> p (a d)")


def prepare(nc, allocators, x, w01, b01, residual, v1p, ident_f, ident_h,
            f32, f16, bf16, i32, ALU, ACT, AX, ds):
    with ExitStack() as ctx:
        sb, pb, sem = allocators(ctx)
        X = sb("X", [P, TILES, D], f32)
        XN = sb("XN", [P, GT, D], f32)
        Y = sb("Y", [P, GT, D], f32)
        W = sb("W", [P, 2, D + DN], f32)
        bias = sb("bias", [P, D + DN], f32)
        stats = sb("stats", [P, TILES, 6], f32)
        moments = sb("moments", [P, TILES, 2], f32)
        rstd = sb("rstd", [P, TILES], f32)
        eps = sb("eps", [P, 1], f32)
        xT = sb("xT", [P, 2, GN], f32)
        v1 = sb("v1", [P, GT, DN], f32)
        rest = sb("rest", [P, GT, DN], f32)
        tps = pb("tps", [P, 2, GN], f32)
        vps = pb("vps", [P, GT, 512], f32)

        x_in, w_in = sem("x_in"), sem("w_in")
        consts, stats_ok, sqrt_ok, rstd_ok = sem("consts"), sem("stats_ok"), sem("sqrt_ok"), sem("rstd_ok")
        xn_ok, tps_ok, xT_ok, vps_ok = sem("xn_ok"), sem("tps_ok"), sem("xT_ok"), sem("vps_ok")
        vps_read, v1_ok, hi_ok, rest_ok, mid_ok = (sem("vps_read"), sem("v1_ok"), sem("hi_ok"),
                                                  sem("rest_ok"), sem("mid_ok"))
        v1_used, res_ok, res_out, dve_own, pool_own = (sem("v1_used"), sem("res_ok"), sem("res_out"),
                                                       sem("dve_own"), sem("pool_own"))
        vps_free, dve_turn, act_turn, pool_turn = sem("vps_free"), sem("dve_turn"), sem("act_turn"), sem("pool_turn")
        block = ctx.enter_context(nc.Block())
        x_t = x.rearrange("(t p) d -> p t d", p=P)
        res_t = residual.rearrange("(t p) d -> p t d", p=P)

        @block.sync
        def _(sp):
            sp.dma_start(X[:, 0:GT, :], x_t[:, 0:GT, :]).then_inc(x_in, 16)
            sp.dma_start(W[:, :, :], w01.rearrange("(k p) n -> p k n", p=P)).then_inc(w_in, 16)
            sp.dma_start(bias[:, :], b01.rearrange("(a n) -> a n", a=1).to_broadcast([P, D + DN])).then_inc(w_in, 16)
            with sp.Fori(1, GROUPS) as g:
                sp.wait_ge(x_in, g * 16)
                sp.dma_start(X[:, ds(g * GT, GT), :], x_t[:, ds(g * GT, GT), :]).then_inc(x_in, 16)
            with sp.Fori(0, GROUPS) as g:
                sp.wait_ge(res_ok, g + 1)
                sp.dma_start(res_t[:, ds(g * GT, GT), :], X[:, ds(g * GT, GT), :]).then_inc(res_out, 16)
            sp.wait_ge(res_out, GROUPS * 16)

        @block.gpsimd
        def _(pool):
            pool.memset(eps[:, :], EPS).then_inc(consts, 1)
            pool.memset(ident_f[:, :], 0.0).then_inc(pool_own, 1)
            pool.wait_ge(pool_own, 1)
            pool.affine_select(out=ident_f[:, :], in_=ident_f[:, :], compare_op=ALU.not_equal, fill=1.0,
                               base=0, pattern=[[-1, P]], channel_multiplier=1).then_inc(pool_own, 1)
            pool.wait_ge(pool_own, 2)
            pool.tensor_copy(ident_h[:, :], ident_f[:, :]).then_inc(consts, 1)
            with pool.Fori(0, GROUPS) as g:
                pool.wait_ge(hi_ok, g + 1)
                pool.sem_inc(pool_turn, 1)
                pool.tensor_tensor(rest[:, :, :], v1[:, :, :], v1p[:, 0, ds(g * GT, GT), :],
                                   ALU.subtract).then_inc(rest_ok, 1)
                pool.wait_ge(mid_ok, g + 1)
                pool.sem_inc(pool_turn, 1)
                pool.tensor_tensor(v1p[:, 2, ds(g * GT, GT), :], rest[:, :, :], v1p[:, 1, ds(g * GT, GT), :],
                                   ALU.subtract).then_inc(v1_used, 1)

        @block.vector
        def _(dve):
            with dve.Fori(0, GROUPS) as g:
                dve.wait_ge(x_in, g * 16 + 16)
                for u in range(GT):
                    nc.vector.bn_stats(stats[:, ds(g * GT + u, 1), :].rearrange("p a s -> p (a s)"),
                                       X[:, ds(g * GT + u, 1), :].rearrange("p a d -> p (a d)")).then_inc(dve_own, 1)
            dve.wait_ge(dve_own, TILES)
            for t in range(TILES):
                nc.vector.bn_aggr(moments[:, t, :], stats[:, t, :]).then_inc(stats_ok, 1)
            dve.wait_ge(sqrt_ok, 1)
            nc.vector.reciprocal(rstd[:, :], rstd[:, :]).then_inc(rstd_ok, 1)
            dve.wait_ge(rstd_ok, 1)
            dve.wait_ge(w_in, 32)

            def normalise(g):
                for u in range(GT):
                    last = nc.vector.tensor_scalar(XN[:, u, :], flat2(X[:, ds(g * GT + u, 1), :]),
                                                   flat2(moments[:, ds(g * GT + u, 1), 0:1]), rstd[:, ds(g * GT + u, 1)],
                                                   ALU.subtract, ALU.mult)
                last.then_inc(xn_ok, 1)

            def finish(g):
                dve.wait_ge(vps_ok, g + 1)
                for u in range(GT):
                    nc.vector.tensor_tensor(Y[:, u, :], vps[:, u, 0:D], bias[:, 0:D], ALU.add).then_inc(dve_own, 1)
                dve.wait_ge(v1_used, g + 1)
                for u in range(GT):
                    last = nc.vector.tensor_tensor(v1[:, u, :], vps[:, u, D:D + DN], bias[:, D:D + DN], ALU.add)
                last.then_inc(v1_ok, 1)
                dve.wait_ge(v1_ok, g + 1)
                dve.sem_inc(vps_free, 1)
                dve.wait_ge(dve_own, g * GT + (TILES + GT))
                nc.vector.tensor_tensor(X[:, ds(g * GT, GT), :], X[:, ds(g * GT, GT), :], Y[:, :, :],
                                        ALU.add).then_inc(res_ok, 1)
                dve.wait_ge(res_ok, g + 1)

            normalise(0)
            with dve.Fori(0, GROUPS - 1) as g:
                dve.wait_ge(tps_ok, g + 1)
                dve.sem_inc(dve_turn, 1)
                normalise(g + 1)
                finish(g)
            finish(GROUPS - 1)

        @block.scalar
        def _(act):
            act.wait_ge(stats_ok, TILES)
            act.wait_ge(consts, 1)
            nc.scalar.activation(rstd[:, :], moments[:, :, 1], ACT.Sqrt, bias=eps[:, 0:1]).then_inc(sqrt_ok, 1)
            act.sem_inc(v1_used, 1)
            with act.Fori(0, GROUPS) as g:
                act.wait_ge(tps_ok, g + 1)
                nc.scalar.copy(xT[:, :, :], tps[:, :, :]).then_inc(xT_ok, 1)
                act.wait_ge(v1_ok, g + 1)
                act.sem_inc(act_turn, 1)
                nc.scalar.copy(v1p[:, 0, ds(g * GT, GT), :], v1[:, :, :]).then_inc(hi_ok, 1)
                act.wait_ge(rest_ok, g + 1)
                act.sem_inc(act_turn, 1)
                nc.scalar.copy(v1p[:, 1, ds(g * GT, GT), :], rest[:, :, :]).then_inc(mid_ok, 1)

        @block.tensor
        def _(pe):
            pe.wait_ge(consts, 2)
            pe.wait_ge(w_in, 32)
            pe.sem_inc(vps_free, 1)
            with pe.Fori(0, GROUPS) as g:
                pe.wait_ge(xn_ok, g + 1)
                for u in range(GT):
                    for k in range(2):
                        last = nc.tensor.transpose(tps[:, k, u * P:(u + 1) * P],
                                                   XN[:, u, k * P:(k + 1) * P],
                                                   ident_f[:, :])
                last.then_inc(tps_ok, 1)
                pe.wait_ge(xT_ok, g + 1)
                pe.wait_ge(vps_free, g + 1)
                for u in range(GT):
                    for k in range(2):
                        last = nc.tensor.matmul(vps[:, u, 0:D + DN], xT[:, k, u * P:(u + 1) * P], W[:, k, :],
                                                start=(k == 0), stop=(k == 1))
                last.then_inc(vps_ok, 1)


def graph(nc, allocators, src_cols, dst_cols, dst_chunks, span_lo, span_hi, chunk_min, chunk_max, v1p, sumT, ident_h,
          f32, f16, bf16, i32, ALU, ACT, AX, ds):
    with ExitStack() as ctx:
        sb, pb, sem = allocators(ctx)
        counts = sb("counts", [P, SRC_PAD, GN], f16)
        countsT = sb("countsT", [P, 2, GT, GN], f16)
        src_hot = sb("src_hot", [P, RING * P], f16)
        pair_hot = sb("pair_hot", [P, RING * WCOL], f16)
        row_code = sb("row_code", [P, CHUNKS_PAD], f32)
        col_code = sb("col_code", [P, CHUNKS_PAD], f32)
        iota_row = sb("iota_row", [P, P], f16)
        iota_col = sb("iota_col", [P, WCOL], f16)
        win_row = sb("win_row", [P, WIN_PAD], f32)
        win_col = sb("win_col", [P, WIN_PAD], f32)
        stage = sb("stage", [P, 2, GN], f32)
        lo_f = sb("lo_f", [1, WINDOWS], f32)
        hi_f = sb("hi_f", [1, WINDOWS], f32)
        tmp_a = sb("tmp_a", [1, WINDOWS], f32)
        tmp_b = sb("tmp_b", [1, WINDOWS], f32)
        ranges = sb("ranges", [1, WINDOWS * 2], i32)
        longest = sb("longest", [1, 2], f32)
        longest_i = sb("longest_i", [1, 2], i32)
        zeros = sb("zeros", [P, P], f16)
        big = pb("big", [P, 4, 512], f32)
        res = pb("res", [P, 2, 512], f32)

        flat = counts[:, :, :].rearrange("p a b -> p (a b)")
        taken = [0]

        def take(n, dt):
            taken[0] += n
            return flat.bitcast(dt)[:, taken[0] - n:taken[0]]

        src_i, dst_i, part_a, part_b, dst_by_chunk = (take(CHUNKS_PAD, i32) for _ in range(5))
        win_i, iota_i, after_i = take(WIN_PAD, i32), take(WCOL, i32), take(CHUNKS, i32)
        min_row, max_row, after, before, found = (take(CHUNKS, f32) for _ in range(5))
        dst_f = take(CHUNKS_PAD, f32)
        ends = take(2 * CHUNK_TILES, f32)
        first_node = take(2 * WIN_TILES, f32)
        spans = take(2 * WIN_TILES, f32)

        edges_in, iotas, own, ends_ok, ends_out, rows_in = (sem("edges_in"), sem("iotas"), sem("own"),
                                                           sem("ends_ok"), sem("ends_out"), sem("rows_in"))
        spans_ok, spans_out, spans_in = sem("spans_ok"), sem("spans_out"), sem("spans_in")
        ranges_ok, longest_ok, ranges_used = sem("ranges_ok"), sem("longest_ok"), sem("ranges_used")
        hot_ok, hot_free, win_ok, win_free = sem("hot_ok"), sem("hot_free"), sem("win_ok"), sem("win_free")
        turned_ok, copied_a, copied_d = sem("turned_ok"), sem("copied_a"), sem("copied_d")
        res_ok, stage_ok, stage_free, zeroed = sem("g_res_ok"), sem("stage_ok"), sem("stage_free"), sem("zeroed")
        pe_turn, act_turn, dve_turn, pool_turn = (sem("g_pe_turn"), sem("g_act_turn"), sem("g_dve_turn"),
                                                  sem("g_pool_turn"))
        block = ctx.enter_context(nc.Block())

        def passes(eng):
            eng.wait_ge(longest_ok, 1)
            n = eng.value_load(longest_i[0:1, 0:1], min_val=1, max_val=CHUNKS + 2)
            return eng.snap((n + (SUB - 1)) // SUB, min_val=1, max_val=CHUNKS // SUB + 1)

        def window_range(eng, w):
            lo = eng.value_load(ranges[0:1, ds(w * 2, 1)], min_val=0, max_val=CHUNKS)
            hi = eng.value_load(ranges[0:1, ds(w * 2 + 1, 1)], min_val=2, max_val=CHUNKS + 2)
            return lo, hi

        @block.sync
        def _(sp):
            sp.dma_start(dst_by_chunk.rearrange("p (c e) -> p c e", e=P),
                         dst_chunks.rearrange("(c p) e -> p c e", p=P)).then_inc(edges_in, 16)
            sp.dma_start(dst_i, dst_cols[:, :]).then_inc(edges_in, 16)
            sp.dma_start(src_i, src_cols[:, :]).then_inc(edges_in, 16)
            sp.wait_ge(ends_ok, 1)
            with nc.allow_non_contiguous_dma(reason="a word per chunk, once"):
                sp.dma_start(chunk_min.rearrange("(c p) -> p c", p=P), ends[:, 0:CHUNK_TILES]).then_inc(ends_out, 16)
                sp.dma_start(chunk_max.rearrange("(c p) -> p c", p=P), ends[:, CHUNK_TILES:]).then_inc(ends_out, 16)
            sp.wait_ge(ends_out, 32)
            sp.dma_start(min_row, chunk_min[0:CHUNKS].rearrange("(a n) -> a n", a=1).to_broadcast([P, CHUNKS])).then_inc(rows_in, 16)
            sp.dma_start(max_row, chunk_max[0:CHUNKS].rearrange("(a n) -> a n", a=1).to_broadcast([P, CHUNKS])).then_inc(rows_in, 16)
            sp.wait_ge(spans_ok, 1)
            with nc.allow_non_contiguous_dma(reason="a word per window, once"):
                sp.dma_start(span_lo.rearrange("(c p) -> p c", p=P), spans[:, 0:WIN_TILES]).then_inc(spans_out, 16)
                sp.dma_start(span_hi.rearrange("(c p) -> p c", p=P), spans[:, WIN_TILES:]).then_inc(spans_out, 16)
            sp.wait_ge(spans_out, 32)
            sp.dma_start(lo_f[:, :], span_lo[0:WINDOWS].rearrange("(a n) -> a n", a=1)).then_inc(spans_in, 16)
            sp.dma_start(hi_f[:, :], span_hi[0:WINDOWS].rearrange("(a n) -> a n", a=1)).then_inc(spans_in, 16)

        @block.gpsimd
        def _(pool):
            pool.memset(zeros[:, :], 0.0).then_inc(zeroed, 1)
            pool.iota(iota_i, [[1, WCOL]], base=0, channel_multiplier=0).then_inc(iotas, 1)
            pool.iota(win_i, [[1, WIN_PAD]], base=0, channel_multiplier=0).then_inc(iotas, 1)
            pool.iota(after_i, [[1, CHUNKS]], base=1, channel_multiplier=0).then_inc(iotas, 1)
            pool.iota(part_a[:, 0:WIN_TILES], [[P * WIN, WIN_TILES]], base=0, channel_multiplier=WIN).then_inc(iotas, 1)
            pool.memset(sumT[:, :], 0.0).then_inc(stage_free, 2)
            n_pass = passes(pool)
            with pool.Fori(0, n_pass) as r:
                with pool.Fori(0, GROUPS) as g:
                    done = pool.snap((r * GROUPS + g) * RESULTS)

                    def add(k, node0, n, slot):
                        pool.wait_ge(stage_ok, done + (k + 3))
                        pool.wait_ge(stage_free, done + (k + 2))
                        pool.sem_inc(pool_turn, 1)
                        pool.tensor_tensor(sumT[:, ds(node0, n)], sumT[:, ds(node0, n)], stage[:, slot, 0:n],
                                           ALU.add).then_inc(stage_free, 1)

                    add(0, g * GN, GN, 0)
                    with pool.Fori(0, PAIRS) as q:
                        for s in range(2):
                            add(q * 2 + (s + 1), q * (2 * GN) + s * GN, GN, (s + 1) % 2)
                    add(BLOCKS, 2 * PAIRS * GN, P, BLOCKS % 2)

        @block.vector
        def _(dve):
            step = Steps(dve, own)

            def then(ins):
                step.done(ins)
                step.wait()

            dve.wait_ge(iotas, 4)
            dve.wait_ge(edges_in, 48)
            nc.vector.tensor_copy(iota_row[:, :], iota_i[:, 0:P])
            nc.vector.tensor_copy(iota_col[:, :], iota_i)
            nc.vector.tensor_scalar(win_row[:, :], win_i, -float(P), None, ALU.mult)
            nc.vector.tensor_scalar(win_col[:, :], win_i, -float(WIN), None, ALU.mult)
            nc.vector.tensor_scalar(first_node[:, 0:WIN_TILES], part_a[:, 0:WIN_TILES], 1.0, None, ALU.mult)
            nc.vector.tensor_scalar(first_node[:, WIN_TILES:], part_a[:, 0:WIN_TILES], float(WIN), None, ALU.add)
            nc.vector.tensor_copy(after, after_i)
            then(nc.vector.tensor_copy(dst_f, dst_by_chunk))
            by_chunk = dst_f.rearrange("p (c e) -> p c e", e=P)
            nc.vector.tensor_reduce(out=ends[:, 0:CHUNK_TILES], in_=by_chunk, op=ALU.min, axis=AX.X)
            nc.vector.tensor_reduce(out=ends[:, CHUNK_TILES:], in_=by_chunk, op=ALU.max, axis=AX.X).then_inc(ends_ok, 1)
            nc.vector.tensor_scalar(before, after, -1.0, float(CHUNKS + 1), ALU.mult, ALU.add)
            nc.vector.tensor_single_scalar(part_a, src_i, P - 1, ALU.bitwise_and)
            then(nc.vector.tensor_single_scalar(part_b, dst_i, 4, ALU.arith_shift_right))
            then(nc.vector.scalar_tensor_tensor(row_code[:, :], part_b, float(P), part_a, ALU.mult, ALU.add))
            then(nc.vector.tensor_single_scalar(part_a, src_i, 7, ALU.arith_shift_right))
            then(nc.vector.scalar_tensor_tensor(col_code[:, :], part_a, float(WIN), dst_i, ALU.mult, ALU.add))
            dve.wait_ge(rows_in, 32)
            for q in range(WIN_TILES):
                then(nc.vector.scalar_tensor_tensor(found, max_row, first_node[:, q:q + 1], before, ALU.is_ge, ALU.mult))
                then(nc.vector.tensor_reduce(out=spans[:, q:q + 1], in_=found, op=ALU.max, axis=AX.X))
                then(nc.vector.scalar_tensor_tensor(found, min_row, first_node[:, WIN_TILES + q:WIN_TILES + q + 1],
                                                    after, ALU.is_lt, ALU.mult))
                then(nc.vector.tensor_reduce(out=spans[:, WIN_TILES + q:WIN_TILES + q + 1], in_=found,
                                             op=ALU.max, axis=AX.X))
            nc.vector.tensor_scalar(spans[:, 0:WIN_TILES], spans[:, 0:WIN_TILES], -1.0, float(CHUNKS),
                                    ALU.mult, ALU.add).then_inc(spans_ok, 1)
            dve.wait_ge(spans_in, 32)
            then(nc.vector.tensor_tensor(tmp_a[:, :], hi_f[:, :], lo_f[:, :], ALU.subtract))
            then(nc.vector.tensor_reduce(out=longest[:, 0:1], in_=tmp_a[:, :], op=ALU.max, axis=AX.X))
            then(nc.vector.tensor_scalar(longest[:, 1:2], longest[:, 0:1], 1.0, None, ALU.max))
            nc.vector.tensor_copy(longest_i[:, 0:1], longest[:, 1:2]).then_inc(longest_ok, 1)
            before_passes = step.n
            n_pass = passes(dve)
            count = dve.alloc_register("hot_count")
            slot = dve.alloc_register("hot_slot")
            dve.reg_mov(count, 0)
            table = ranges[:, :].rearrange("p (w two) -> p w two", two=2)
            with dve.Fori(0, n_pass) as r:
                step.at(r * 10 + before_passes)
                dve.wait_ge(ranges_used, r + 1)
                then(nc.vector.tensor_tensor(tmp_a[:, :], lo_f[:, :], hi_f[:, :], ALU.is_lt))
                then(nc.vector.tensor_scalar(tmp_b[:, :], lo_f[:, :], float(-CHUNKS), None, ALU.add))
                then(nc.vector.tensor_tensor(tmp_b[:, :], tmp_b[:, :], tmp_a[:, :], ALU.mult))
                then(nc.vector.tensor_scalar(table[:, :, 0], tmp_b[:, :], float(CHUNKS), None, ALU.add))
                then(nc.vector.tensor_scalar(tmp_b[:, :], lo_f[:, :], 2.0, None, ALU.add))
                then(nc.vector.tensor_tensor(tmp_b[:, :], tmp_b[:, :], hi_f[:, :], ALU.max))
                then(nc.vector.tensor_scalar(lo_f[:, :], lo_f[:, :], float(SUB), None, ALU.add))
                then(nc.vector.tensor_tensor(tmp_b[:, :], tmp_b[:, :], lo_f[:, :], ALU.min))
                then(nc.vector.tensor_scalar(tmp_b[:, :], tmp_b[:, :], float(-(CHUNKS + 2)), None, ALU.add))
                then(nc.vector.tensor_tensor(tmp_b[:, :], tmp_b[:, :], tmp_a[:, :], ALU.mult))
                nc.vector.tensor_scalar(table[:, :, 1], tmp_b[:, :], float(CHUNKS + 2), None, ALU.add).then_inc(ranges_ok, 1)
                dve.wait_ge(ranges_ok, r + 1)
                dve.sem_inc(dve_turn, 1)
                with dve.Fori(0, GROUPS) as g:
                    with dve.Fori(0, WPG) as j:
                        w = dve.snap(g * WPG + j, min_val=0, max_val=WINDOWS - 1)
                        lo, hi = window_range(dve, w)
                        with dve.Fori(lo, hi) as c_any:
                            c = dve.snap(c_any, min_val=0, max_val=CHUNKS + 1)
                            dve.reg_alu(slot, count, RING - 1, ALU.bitwise_and)
                            s = dve.snap(slot, min_val=0, max_val=RING - 1)
                            dve.reg_add(count, count, 1)
                            dve.wait_ge(hot_free, dve.snap(count))
                            dve.sem_inc(dve_turn, 1)
                            nc.vector.tensor_scalar(src_hot[:, ds(s * P, P)], iota_row[:, :], row_code[:, ds(c, 1)],
                                                    win_row[:, ds(w, 1)], ALU.subtract, ALU.is_equal).then_inc(hot_ok, 1)
                            nc.vector.tensor_scalar(pair_hot[:, ds(s * WCOL, WCOL)], iota_col[:, :],
                                                    col_code[:, ds(c, 1)], win_col[:, ds(w, 1)],
                                                    ALU.subtract, ALU.is_equal).then_inc(hot_ok, 1)
                    turned = dve.snap((r * GROUPS + g) * BLOCKS)

                    def copy(b, s, n):
                        dve.wait_ge(turned_ok, turned + (b + 1))
                        nc.vector.tensor_copy(countsT[:, s, 0:2, 0:n], big[:, 0:2, 0:n]).then_inc(copied_d, 1)

                    with dve.Fori(0, PAIRS) as q:
                        for s in range(2):
                            copy(q * 2 + s, s, GN)
                    copy(2 * PAIRS, 0, P)

        @block.scalar
        def _(act):
            act.sem_inc(win_free, 2)
            n_pass = passes(act)
            with act.Fori(0, n_pass) as r:
                with act.Fori(0, GROUPS) as g:
                    group = act.snap(r * GROUPS + g)
                    with act.Fori(0, WPG // 2) as j:
                        for s in range(2):
                            act.wait_ge(win_ok, group * WPG + j * 2 + (s + 1))
                            act.sem_inc(act_turn, 1)
                            nc.scalar.copy(counts[:, :, ds(j * (2 * WIN) + s * WIN, WIN)].rearrange("p (b h) w -> p b h w", b=2),
                                           big[:, 2 * s:2 * s + 2, 0:HALF].rearrange("p b (h w) -> p b h w", w=WIN)
                                           ).then_inc(win_free, 1)

                    def copy(b, s, n):
                        act.wait_ge(turned_ok, group * BLOCKS + (b + 1))
                        nc.scalar.copy(countsT[:, s, 2:4, 0:n], big[:, 2:4, 0:n]).then_inc(copied_a, 1)

                    def result(k, slot, n):
                        act.wait_ge(res_ok, group * RESULTS + (k + 1))
                        act.wait_ge(stage_free, group * RESULTS + (k + 1))
                        nc.scalar.copy(stage[:, slot, 0:n], res[:, slot, 0:n]).then_inc(stage_ok, 1)

                    with act.Fori(0, PAIRS) as q:
                        for s in range(2):
                            copy(q * 2 + s, s, GN)
                            result(q * 2 + s, s, GN)
                    copy(2 * PAIRS, 0, P)
                    result(2 * PAIRS, 0, GN)
                    result(BLOCKS, 1, P)

        @block.tensor
        def _(pe):
            pe.wait_ge(zeroed, 1)
            pe.sem_inc(hot_free, RING)
            pe.sem_inc(copied_a, 1)
            pe.sem_inc(copied_d, 1)
            pe.sem_inc(stage_ok, 2)
            pe.sem_inc(ranges_used, 1)
            n_pass = passes(pe)
            count = pe.alloc_register("hot_seen")
            slot = pe.alloc_register("hot_slot_pe")
            pe.reg_mov(count, 0)
            with pe.Fori(0, n_pass) as r:
                pe.wait_ge(ranges_ok, r + 1)
                pe.sem_inc(pe_turn, 1)
                with pe.Fori(0, GROUPS) as g:
                    group = pe.snap(r * GROUPS + g)
                    pe.wait_ge(copied_a, group * BLOCKS + 1)
                    pe.wait_ge(copied_d, group * BLOCKS + 1)
                    pe.sem_inc(pe_turn, 1)
                    with pe.Fori(0, WPG // 2) as j:
                        for half in range(2):
                            w = pe.snap(g * WPG + j * 2 + half, min_val=0, max_val=WINDOWS - 1)
                            lo, hi = window_range(pe, w)
                            pe.wait_ge(win_free, group * WPG + j * 2 + (half + 1))

                            def item(start):
                                pe.reg_alu(slot, count, RING - 1, ALU.bitwise_and)
                                s = pe.snap(slot, min_val=0, max_val=RING - 1)
                                pe.reg_add(count, count, 1)
                                pe.wait_ge(hot_ok, pe.snap(count) * 2)
                                pe.sem_inc(pe_turn, 1)
                                for b in range(2):
                                    last = nc.tensor.matmul(big[:, 2 * half + b, 0:HALF], src_hot[:, ds(s * P, P)],
                                                            pair_hot[:, ds(s * WCOL + b * HALF, HALF)],
                                                            start=start, stop=False)
                                last.then_inc(hot_free, 1)

                            item(True)
                            with pe.Fori(lo + 1, hi) as c:
                                item(False)
                            for b in range(2):
                                last = nc.tensor.matmul(big[:, 2 * half + b, 0:1], zeros[:, :], zeros[:, 0:1],
                                                        start=False, stop=True)
                            last.then_inc(win_ok, 1)

                    def turn(b, n_src):
                        for u in range(n_src):
                            for t in range(GT):
                                last = nc.tensor.matmul(big[:, t, u * P:(u + 1) * P],
                                                        counts[:, ds(b * GT + u, 1), t * P:(t + 1) * P].rearrange("p a n -> p (a n)"),
                                                        ident_h[:, :], start=True, stop=True)
                        last.then_inc(turned_ok, 1)

                    def to_sources(b, s, k, slot, n):
                        pe.wait_ge(copied_a, group * BLOCKS + (b + 2))
                        pe.wait_ge(copied_d, group * BLOCKS + (b + 2))
                        pe.wait_ge(stage_ok, group * RESULTS + (k + 1))
                        pe.sem_inc(pe_turn, 1)
                        for t in range(GT):
                            for part in range(PARTS):
                                last = nc.tensor.matmul(res[:, slot, 0:n],
                                                        v1p[:, part, ds(g * GT + t, 1), :].rearrange("p a n -> p (a n)"),
                                                        countsT[:, s, t, 0:n],
                                                        start=(t == 0 and part == 0), stop=(t == GT - 1 and part == PARTS - 1))
                        last.then_inc(res_ok, 1)

                    pe.wait_ge(win_free, group * WPG + (WPG + 2))
                    pe.sem_inc(pe_turn, 1)
                    turn(0, GT)
                    pe.wait_ge(stage_ok, group * RESULTS + 1)
                    pe.sem_inc(pe_turn, 1)

                    def to_destinations(h, first, final):
                        for part in range(PARTS):
                            last = nc.tensor.matmul(res[:, 0, :], v1p[:, part, ds(h, 1), :].rearrange("p a n -> p (a n)"),
                                                    counts[:, ds(h, 1), :].rearrange("p a n -> p (a n)"),
                                                    start=(first and part == 0), stop=(final and part == PARTS - 1))
                        return last

                    to_destinations(0, True, False)
                    with pe.Fori(0, (SRC_TILES - 1) // GT - 1) as q:
                        for u in range(GT):
                            to_destinations(q * GT + (u + 1), False, False)
                    for u in range(GT):
                        last = to_destinations(SRC_TILES - GT + u, False, u == GT - 1)
                    last.then_inc(res_ok, 1)

                    def turn_next(b, n_src):
                        pe.wait_ge(copied_a, group * BLOCKS + (b + 1))
                        pe.wait_ge(copied_d, group * BLOCKS + (b + 1))
                        pe.sem_inc(pe_turn, 1)
                        turn(b, n_src)

                    with pe.Fori(0, PAIRS - 1) as q:
                        for s in range(2):
                            turn_next(q * 2 + (s + 1), GT)
                            to_sources(q * 2 + s, s, q * 2 + (s + 1), (s + 1) % 2, GN)
                    turn_next(2 * PAIRS - 1, GT)
                    to_sources(2 * PAIRS - 2, 0, 2 * PAIRS - 1, 1, GN)
                    turn_next(2 * PAIRS, 1)
                    to_sources(2 * PAIRS - 1, 1, 2 * PAIRS, 0, GN)
                    to_sources(2 * PAIRS, 0, BLOCKS, 1, P)
                pe.sem_inc(ranges_used, 1)


def ffn(nc, allocators, residual, sumT, ident_f, W1, b1, Wg, bg, Wd, bd, out,
        f32, f16, bf16, i32, ALU, ACT, AX, ds):
    K1, KH = D // P, HID // P
    with ExitStack() as ctx:
        sb, pb, sem = allocators(ctx)
        X = sb("fX", [P, 2, GT, D], f32)
        XN = sb("fXN", [P, GT, D], f32)
        nbT = sb("nbT", [P, GN], f32)
        w1 = sb("w1", [P, K1, HID], f32)
        wg = sb("wg", [P, KH, EXPERTS], f32)
        wd = sb("wd", [P, KH, EXPERTS * D], f32)
        b1c = sb("b1c", [P, KH], f32)
        bgr = sb("bgr", [P, EXPERTS], f32)
        bdr = sb("bdr", [P, EXPERTS * D], f32)
        rank = sb("rank", [P, GT, EXPERTS], f32)
        rank_i = sb("rank_i", [P, GT * EXPERTS], i32)
        eps = sb("f_eps", [P, 1], f32)
        stats = sb("f_stats", [P, GT, 6], f32)
        mv = sb("f_mv", [P, GT, 2], f32)
        std = sb("std", [P, GT], f32)
        rstd = sb("f_rstd", [P, GT], f32)
        xT = sb("f_xT", [P, K1, GN], f32)
        H = sb("H", [P, KH, GN], f32)
        logits = sb("logits", [P, GT, EXPERTS], f32)
        shifted = sb("shifted", [P, GT, EXPERTS], f32)
        expo = sb("expo", [P, GT, EXPERTS], f32)
        top = sb("top", [P, GT], f32)
        total = sb("total", [P, GT], f32)
        coef = sb("coef", [P, GT, EXPERTS], f32)
        bias_y = sb("bias_y", [P, 2, D], f32)
        up = pb("up", [P, 2, 512], f32)
        gate = pb("gate", [P, GT, EXPERTS], f32)
        down = pb("down", [P, 4, 512], f32)

        x_in, w_in, consts, own, y_out = sem("f_x_in"), sem("f_w_in"), sem("f_consts"), sem("f_own"), sem("y_out")
        nb_ok, nb_used, var_ok, std_ok, xn_ok = sem("nb_ok"), sem("nb_used"), sem("var_ok"), sem("std_ok"), sem("f_xn_ok")
        xT_turn, xT_ok, up_ok, h_ok, gate_ok = sem("xT_turn"), sem("f_xT_ok"), sem("up_ok"), sem("h_ok"), sem("gate_ok")
        shift_ok, exp_ok, down_ok, down_used = sem("shift_ok"), sem("exp_ok"), sem("down_ok"), sem("down_used")
        y_ok, pool_own, nb_in, nb_free, pool_turn = (sem("y_ok"), sem("f_pool_own"), sem("nb_in"), sem("nb_free"),
                                                    sem("f_pool_turn"))
        pe_turn, act_turn, dve_turn = sem("f_pe_turn"), sem("f_act_turn"), sem("f_dve_turn")
        block = ctx.enter_context(nc.Block())
        res_t = residual.rearrange("(t p) d -> p t d", p=P)
        out_t = out.rearrange("(t p) d -> p t d", p=P)

        def row(a, n):
            return a.rearrange("(a n) -> a n", a=1).to_broadcast([P, n])

        @block.sync
        def _(sp):
            sp.dma_start(X[:, 0, :, :], res_t[:, 0:GT, :]).then_inc(x_in, 16)
            sp.dma_start(w1[:, :, :], W1.rearrange("(k p) n -> p k n", p=P)).then_inc(w_in, 16)
            with nc.allow_non_contiguous_dma(reason="a word per hidden feature, once"):
                sp.dma_start(b1c[:, :], b1.rearrange("(k p) -> p k", p=P)).then_inc(w_in, 16)
            sp.dma_start(wg[:, :, :], Wg.rearrange("(k p) n -> p k n", p=P)).then_inc(w_in, 16)
            sp.dma_start(bgr[:, :], row(bg, EXPERTS)).then_inc(w_in, 16)
            sp.dma_start(bdr[:, :], row(bd.rearrange("e d -> (e d)"), EXPERTS * D)).then_inc(w_in, 16)
            for e in range(EXPERTS):
                sp.dma_start(wd[:, :, e * D:(e + 1) * D], Wd[e, :, :].rearrange("(k p) n -> p k n", p=P)).then_inc(w_in, 16)
            with sp.Fori(1, GROUPS) as g:
                sp.wait_ge(y_out, g * 16)
                sp.sem_inc(dve_turn, 1)
                sp.dma_start(X[:, ds(g % 2, 1), :, :].rearrange("p a t d -> p (a t) d"), res_t[:, ds(g * GT, GT), :]).then_inc(x_in, 16)

        @block.gpsimd
        def _(pool):
            pool.memset(eps[:, :], EPS).then_inc(consts, 1)
            pool.iota(rank_i[:, :], [[0, GT], [-1, EXPERTS]], base=EXPERTS, channel_multiplier=0).then_inc(pool_own, 1)
            pool.wait_ge(pool_own, 1)
            pool.tensor_copy(rank[:, :, :].rearrange("p a e -> p (a e)"), rank_i[:, :]).then_inc(consts, 1)
            pool.sem_inc(nb_free, 1)
            with pool.Fori(0, GROUPS) as g:
                pool.wait_ge(nb_free, g + 1)
                pool.sem_inc(pool_turn, 1)
                pool.tensor_copy(nbT[:, :], sumT[:, ds(g * GN, GN)]).then_inc(nb_in, 1)

        @block.vector
        def _(dve):
            step = Steps(dve, own)

            def then(ins):
                step.done(ins)
                step.wait()

            dve.wait_ge(consts, 2)
            dve.wait_ge(w_in, 16 * (5 + EXPERTS))
            with dve.Fori(0, GROUPS) as g:
                step.at(g * 90)
                slot = dve.snap(g % 2, min_val=0, max_val=1)
                x = [X[:, ds(slot, 1), t, :].rearrange("p a d -> p (a d)") for t in range(GT)]
                dve.wait_ge(x_in, g * 16 + 16)
                dve.wait_ge(nb_ok, g + 1)
                for t in range(GT):
                    last = step.done(nc.vector.tensor_tensor(x[t][:, 0:DN], x[t][:, 0:DN], up[:, 0, t * P:(t + 1) * P], ALU.add))
                step.wait()
                dve.sem_inc(nb_used, 1)
                for t in range(GT):
                    step.done(nc.vector.bn_stats(stats[:, t, :], x[t]))
                step.wait()
                dve.sem_inc(dve_turn, 1)
                for t in range(GT):
                    nc.vector.bn_aggr(mv[:, t, :], stats[:, t, :]).then_inc(var_ok, 1)
                dve.wait_ge(std_ok, g + 1)
                then(nc.vector.reciprocal(rstd[:, :], std[:, :]))
                for t in range(GT):
                    last = nc.vector.tensor_scalar(XN[:, t, :], x[t], mv[:, t, 0:1], rstd[:, t:t + 1], ALU.subtract, ALU.mult)
                last.then_inc(xn_ok, 1)
                dve.wait_ge(gate_ok, g + 1)
                for t in range(GT):
                    step.done(nc.vector.tensor_tensor(logits[:, t, :], gate[:, t, :], bgr[:, :], ALU.add))
                step.wait()
                then(nc.vector.tensor_reduce(out=top[:, :], in_=logits[:, :, :], op=ALU.max, axis=AX.X))
                for t in range(GT):
                    last = nc.vector.tensor_scalar(shifted[:, t, :], logits[:, t, :], top[:, t:t + 1], None, ALU.subtract)
                last.then_inc(shift_ok, 1)
                dve.wait_ge(exp_ok, g + 1)
                then(nc.vector.tensor_reduce(out=total[:, :], in_=expo[:, :, :], op=ALU.add, axis=AX.X))
                then(nc.vector.reciprocal(total[:, :], total[:, :]))
                for t in range(GT):
                    step.done(nc.vector.tensor_scalar(expo[:, t, :], expo[:, t, :], total[:, t:t + 1], None, ALU.mult))
                step.wait()
                then(nc.vector.tensor_reduce(out=top[:, :], in_=expo[:, :, :], op=ALU.max, axis=AX.X))
                for t in range(GT):
                    step.done(nc.vector.scalar_tensor_tensor(shifted[:, t, :], expo[:, t, :], top[:, t:t + 1], rank[:, t, :],
                                                             ALU.is_equal, ALU.mult))
                step.wait()
                then(nc.vector.tensor_reduce(out=total[:, :], in_=shifted[:, :, :], op=ALU.max, axis=AX.X))
                for t in range(GT):
                    step.done(nc.vector.scalar_tensor_tensor(coef[:, t, :], shifted[:, t, :], total[:, t:t + 1], expo[:, t, :],
                                                             ALU.is_equal, ALU.mult))
                step.wait()
                for t in range(GT):
                    dve.wait_ge(down_ok, g * GT + (t + 1))
                    for e in range(EXPERTS):
                        part = down[:, e // 2, (e % 2) * D:(e % 2 + 1) * D]
                        then(nc.vector.tensor_tensor(bias_y[:, e % 2, :], part, bdr[:, e * D:(e + 1) * D], ALU.add))
                        ins = nc.vector.scalar_tensor_tensor(x[t], bias_y[:, e % 2, :], coef[:, t, e:e + 1], x[t], ALU.mult, ALU.add)
                        if e == EXPERTS - 1:
                            ins.then_inc(down_used, 1)
                            dve.wait_ge(down_used, g * GT + (t + 2))
                        else:
                            then(ins)
                dve.sem_inc(y_ok, 1)
                assert step.n == 90

        @block.scalar
        def _(act):
            act.wait_ge(consts, 2)
            with act.Fori(0, GROUPS) as g:
                act.wait_ge(var_ok, g * GT + GT)
                nc.scalar.activation(std[:, :], mv[:, :, 1], ACT.Sqrt, bias=eps[:, 0:1]).then_inc(std_ok, 1)
                act.wait_ge(xT_turn, g + 1)
                nc.scalar.copy(xT[:, :, :], up[:, :, :]).then_inc(xT_ok, 1)
                for j in range(KH):
                    act.wait_ge(up_ok, g * KH + (j + 1))
                    nc.scalar.activation(H[:, j, :], up[:, j % 2, :], ACT.Gelu, bias=b1c[:, j:j + 1]).then_inc(h_ok, 1)
                act.wait_ge(shift_ok, g + 1)
                nc.scalar.activation(expo[:, :, :], shifted[:, :, :], ACT.Exp).then_inc(exp_ok, 1)
                act.wait_ge(y_ok, g + 1)
                act.sem_inc(act_turn, 1)
                act.dma_start(out_t[:, ds(g * GT, GT), :], X[:, ds(g % 2, 1), :, :].rearrange("p a t d -> p (a t) d")).then_inc(y_out, 16)
            act.wait_ge(y_out, GROUPS * 16)

        @block.tensor
        def _(pe):
            pe.wait_ge(w_in, 16 * (5 + EXPERTS))
            pe.sem_inc(down_used, 1)
            with pe.Fori(0, GROUPS) as g:
                pe.wait_ge(nb_in, g + 1)
                for t in range(GT):
                    last = nc.tensor.transpose(up[:, 0, t * P:(t + 1) * P], nbT[:, t * P:(t + 1) * P], ident_f[:, :])
                last.then_inc(nb_ok, 1)
                pe.wait_ge(nb_used, g + 1)
                pe.sem_inc(nb_free, 1)
                pe.wait_ge(xn_ok, g + 1)
                for t in range(GT):
                    for k in range(K1):
                        last = nc.tensor.transpose(up[:, k, t * P:(t + 1) * P], XN[:, t, k * P:(k + 1) * P], ident_f[:, :])
                last.then_inc(xT_turn, 1)
                pe.wait_ge(xT_ok, g + 1)
                for j in range(KH):
                    if j >= 2:
                        pe.wait_ge(h_ok, g * KH + (j - 1))
                    for k in range(K1):
                        last = nc.tensor.matmul(up[:, j % 2, :], w1[:, k, j * P:(j + 1) * P], xT[:, k, :],
                                                start=(k == 0), stop=(k == K1 - 1))
                    last.then_inc(up_ok, 1)
                pe.wait_ge(h_ok, g * KH + KH)
                for t in range(GT):
                    for j in range(KH):
                        last = nc.tensor.matmul(gate[:, t, :], H[:, j, t * P:(t + 1) * P], wg[:, j, :],
                                                start=(j == 0), stop=(j == KH - 1))
                last.then_inc(gate_ok, 1)
                for t in range(GT):
                    pe.wait_ge(down_used, g * GT + (t + 1))
                    for b in range(4):
                        for j in range(KH):
                            last = nc.tensor.matmul(down[:, b, :], H[:, j, t * P:(t + 1) * P], wd[:, j, b * 512:(b + 1) * 512],
                                                    start=(j == 0), stop=(j == KH - 1))
                    last.then_inc(down_ok, 1)


def kernel(**inputs):
    import numpy as np
    import concourse.bacc as bacc
    from concourse.bass_utils import run_bass_kernel_spmd

    a = {n: np.asarray(v) for n, v in inputs.items()}
    rows = TILES * P
    edges = CHUNKS_PAD * P
    x = np.concatenate([a["x"], np.zeros((rows - NODES, D), np.float32)])
    src = np.concatenate([a["src"], np.zeros(edges - EDGES, np.int32)]).reshape(CHUNKS_PAD, P)
    dst = np.concatenate([a["dst"], np.full(edges - EDGES, NO_NODE, np.int32)]).reshape(CHUNKS_PAD, P)
    arrays = {
        "x": x,
        "src_cols": np.ascontiguousarray(src.T),
        "dst_cols": np.ascontiguousarray(dst.T),
        "dst_chunks": dst,
        "w01": np.ascontiguousarray(np.concatenate([a["L0_gnn_w0_w"], a["L0_gnn_w1_w"]]).T),
        "b01": np.concatenate([a["L0_gnn_w0_b"], a["L0_gnn_w1_b"]]),
        "W1": a["L0_ffn_W1"], "b1": a["L0_ffn_b1"], "Wg": a["L0_ffn_Wg"], "bg": a["L0_ffn_bg"],
        "Wd": a["L0_ffn_Wd"], "bd": a["L0_ffn_bd"],
    }
    nc = bacc.Bacc("TRN2", target_bir_lowering=False, num_devices=1)
    args = {n: nc.dram_tensor("in_" + n, v.shape, mybir.dt.from_np(v.dtype), kind="ExternalInput").ap()
            for n, v in arrays.items()}
    out = nc.dram_tensor("out", (rows, D), mybir.dt.float32, kind="ExternalOutput").ap()
    build(nc, out=out, **args)
    r = run_bass_kernel_spmd(nc, [{"in_" + n: v for n, v in arrays.items()}], core_ids=[0])
    return r.results[0]["out"][0:NODES]
```

```python
import concourse.bass as bass
from concourse import mybir
from contextlib import ExitStack

P = 128
D = 256
DN = 128
HID = 1024
EXPERTS = 8
NODES = 6250
EDGES = 106250
EPS = 1e-5

TILES = 52
GT = 4
GROUPS = TILES // GT
GN = GT * P
SRC_TILES = 49
SRC_PAD = 50
WIN = 16
CT = 3
BANDS = -(-SRC_TILES // CT)
BN = CT * P
WPB = BN // WIN
WINDOWS = BANDS * WPB
WCOL = SRC_PAD * WIN
HALF = WCOL // 2
BT = 2
BLOCK = BT * P
BLOCKS = SRC_PAD // BT
CHUNKS = -(-EDGES // P)
CHUNK_TILES = -(-CHUNKS // P)
CHUNKS_PAD = CHUNK_TILES * P
WIN_TILES = -(-WINDOWS // P)
WIN_PAD = WIN_TILES * P
NO_NODE = 8192
UNIT = 3
SUB = 5 * UNIT
LOAD = WPB // 2
PARTS = 3
assert WPB == BLOCKS - 1 and BANDS % 2 == 1 and SUB * P <= 2048

K1, KH = D // P, HID // P
SLOT_TILES = (NODES + EXPERTS * (P - 1)) // P
SLOTS = SLOT_TILES * P
NOWHERE = 1 << 16


class Steps:

    def __init__(self, eng, sem):
        self.eng, self.sem, self.base, self.n = eng, sem, 0, 0

    def at(self, base):
        self.base, self.n = base, 0

    def done(self, ins):
        ins.then_inc(self.sem, 1)
        self.n += 1
        return ins

    def wait(self):
        self.eng.wait_ge(self.sem, self.base + self.n)


def build(nc, x, src_cols, dst_cols, dst_chunks, w01, b01, W1, b1, Wg, bg, Wd, bd, out):
    f32, f16, bf16, i32 = (mybir.dt.float32, mybir.dt.float16, mybir.dt.bfloat16, mybir.dt.int32)
    ALU, ACT, AX = mybir.AluOpType, mybir.ActivationFunctionType, mybir.AxisListType
    ds = bass.ds

    with ExitStack() as whole:
        def allocators(ctx):
            return (lambda n, s, d: ctx.enter_context(nc.sbuf_tensor(n, s, d)),
                    lambda n, s, d: ctx.enter_context(nc.psum_tensor(n, s, d)),
                    lambda n: ctx.enter_context(nc.semaphore(n)))

        sb, _, sem = allocators(whole)
        residual = nc.dram_tensor("residual", [TILES * P, D], f32, kind="Internal").ap()
        span_lo = nc.dram_tensor("span_lo", [WIN_PAD], f32, kind="Internal").ap()
        span_hi = nc.dram_tensor("span_hi", [WIN_PAD], f32, kind="Internal").ap()
        chunk_min = nc.dram_tensor("chunk_min", [CHUNKS_PAD], f32, kind="Internal").ap()
        chunk_max = nc.dram_tensor("chunk_max", [CHUNKS_PAD], f32, kind="Internal").ap()
        sumT = sb("sumT", [P, TILES * P], f32)
        ident_f = sb("ident_f", [P, P], f32)
        ident_h = sb("ident_h", [P, P], f16)

        with ExitStack() as front:
            sbf, _, _ = allocators(front)
            v1p = sbf("v1p", [P, PARTS, TILES, DN], bf16)
            prepare(nc, allocators, x, w01, b01, residual, v1p, ident_f, ident_h,
                    f32, f16, bf16, i32, ALU, ACT, AX, ds)
            graph(nc, allocators, src_cols, dst_cols, dst_chunks, span_lo, span_hi, chunk_min, chunk_max, v1p, sumT, ident_h,
                  f32, f16, bf16, i32, ALU, ACT, AX, ds)
        ffn(nc, allocators, residual, sumT, ident_f, W1, b1, Wg, bg, Wd, bd, out,
            f32, f16, bf16, i32, ALU, ACT, AX, ds)


def flat2(ap):
    return ap.rearrange("p a d -> p (a d)")


def prepare(nc, allocators, x, w01, b01, residual, v1p, ident_f, ident_h,
            f32, f16, bf16, i32, ALU, ACT, AX, ds):
    with ExitStack() as ctx:
        sb, pb, sem = allocators(ctx)
        X = sb("X", [P, TILES, D], f32)
        XN = sb("XN", [P, GT, D], f32)
        Y = sb("Y", [P, GT, D], f32)
        W = sb("W", [P, 2, D + DN], f32)
        bias = sb("bias", [P, D + DN], f32)
        stats = sb("stats", [P, TILES, 6], f32)
        moments = sb("moments", [P, TILES, 2], f32)
        rstd = sb("rstd", [P, TILES], f32)
        eps = sb("eps", [P, 1], f32)
        xT = sb("xT", [P, 2, GN], f32)
        v1 = sb("v1", [P, GT, DN], f32)
        rest = sb("rest", [P, GT, DN], f32)
        tps = pb("tps", [P, 2, GN], f32)
        vps = pb("vps", [P, GT, 512], f32)

        x_in, w_in = sem("x_in"), sem("w_in")
        consts, stats_ok, sqrt_ok, rstd_ok = sem("consts"), sem("stats_ok"), sem("sqrt_ok"), sem("rstd_ok")
        xn_ok, tps_ok, xT_ok, vps_ok = sem("xn_ok"), sem("tps_ok"), sem("xT_ok"), sem("vps_ok")
        vps_read, v1_ok, hi_ok, rest_ok, mid_ok = (sem("vps_read"), sem("v1_ok"), sem("hi_ok"),
                                                  sem("rest_ok"), sem("mid_ok"))
        v1_used, res_ok, res_out, dve_own, pool_own = (sem("v1_used"), sem("res_ok"), sem("res_out"),
                                                       sem("dve_own"), sem("pool_own"))
        vps_free, dve_turn, act_turn, pool_turn = sem("vps_free"), sem("dve_turn"), sem("act_turn"), sem("pool_turn")
        block = ctx.enter_context(nc.Block())
        x_t = x.rearrange("(t p) d -> p t d", p=P)
        res_t = residual.rearrange("(t p) d -> p t d", p=P)

        @block.sync
        def _(sp):
            sp.dma_start(X[:, 0:GT, :], x_t[:, 0:GT, :]).then_inc(x_in, 16)
            sp.dma_start(W[:, :, :], w01.rearrange("(k p) n -> p k n", p=P)).then_inc(w_in, 16)
            sp.dma_start(bias[:, :], b01.rearrange("(a n) -> a n", a=1).to_broadcast([P, D + DN])).then_inc(w_in, 16)
            with sp.Fori(1, GROUPS) as g:
                sp.wait_ge(x_in, g * 16)
                sp.dma_start(X[:, ds(g * GT, GT), :], x_t[:, ds(g * GT, GT), :]).then_inc(x_in, 16)
            with sp.Fori(0, GROUPS) as g:
                sp.wait_ge(res_ok, g + 1)
                sp.dma_start(res_t[:, ds(g * GT, GT), :], X[:, ds(g * GT, GT), :]).then_inc(res_out, 16)
            sp.wait_ge(res_out, GROUPS * 16)

        @block.gpsimd
        def _(pool):
            pool.memset(eps[:, :], EPS).then_inc(consts, 1)
            pool.memset(ident_f[:, :], 0.0).then_inc(pool_own, 1)
            pool.wait_ge(pool_own, 1)
            pool.affine_select(out=ident_f[:, :], in_=ident_f[:, :], compare_op=ALU.not_equal, fill=1.0,
                               base=0, pattern=[[-1, P]], channel_multiplier=1).then_inc(pool_own, 1)
            pool.wait_ge(pool_own, 2)
            pool.tensor_copy(ident_h[:, :], ident_f[:, :]).then_inc(consts, 1)
            with pool.Fori(0, GROUPS) as g:
                pool.wait_ge(hi_ok, g + 1)
                pool.sem_inc(pool_turn, 1)
                pool.tensor_tensor(rest[:, :, :], v1[:, :, :], v1p[:, 0, ds(g * GT, GT), :],
                                   ALU.subtract).then_inc(rest_ok, 1)
                pool.wait_ge(mid_ok, g + 1)
                pool.sem_inc(pool_turn, 1)
                pool.tensor_tensor(v1p[:, 2, ds(g * GT, GT), :], rest[:, :, :], v1p[:, 1, ds(g * GT, GT), :],
                                   ALU.subtract).then_inc(v1_used, 1)

        @block.vector
        def _(dve):
            with dve.Fori(0, GROUPS) as g:
                dve.wait_ge(x_in, g * 16 + 16)
                for u in range(GT):
                    nc.vector.bn_stats(stats[:, ds(g * GT + u, 1), :].rearrange("p a s -> p (a s)"),
                                       X[:, ds(g * GT + u, 1), :].rearrange("p a d -> p (a d)")).then_inc(dve_own, 1)
            dve.wait_ge(dve_own, TILES)
            for t in range(TILES):
                nc.vector.bn_aggr(moments[:, t, :], stats[:, t, :]).then_inc(stats_ok, 1)
            dve.wait_ge(sqrt_ok, 1)
            nc.vector.reciprocal(rstd[:, :], rstd[:, :]).then_inc(rstd_ok, 1)
            dve.wait_ge(rstd_ok, 1)
            dve.wait_ge(w_in, 32)

            def normalise(g):
                for u in range(GT):
                    last = nc.vector.tensor_scalar(XN[:, u, :], flat2(X[:, ds(g * GT + u, 1), :]),
                                                   flat2(moments[:, ds(g * GT + u, 1), 0:1]), rstd[:, ds(g * GT + u, 1)],
                                                   ALU.subtract, ALU.mult)
                last.then_inc(xn_ok, 1)

            def finish(g):
                dve.wait_ge(vps_ok, g + 1)
                for u in range(GT):
                    nc.vector.tensor_tensor(Y[:, u, :], vps[:, u, 0:D], bias[:, 0:D], ALU.add).then_inc(dve_own, 1)
                dve.wait_ge(v1_used, g + 1)
                for u in range(GT):
                    last = nc.vector.tensor_tensor(v1[:, u, :], vps[:, u, D:D + DN], bias[:, D:D + DN], ALU.add)
                last.then_inc(v1_ok, 1)
                dve.wait_ge(v1_ok, g + 1)
                dve.sem_inc(vps_free, 1)
                dve.wait_ge(dve_own, g * GT + (TILES + GT))
                nc.vector.tensor_tensor(X[:, ds(g * GT, GT), :], X[:, ds(g * GT, GT), :], Y[:, :, :],
                                        ALU.add).then_inc(res_ok, 1)
                dve.wait_ge(res_ok, g + 1)

            normalise(0)
            with dve.Fori(0, GROUPS - 1) as g:
                dve.wait_ge(tps_ok, g + 1)
                dve.sem_inc(dve_turn, 1)
                normalise(g + 1)
                finish(g)
            finish(GROUPS - 1)

        @block.scalar
        def _(act):
            act.wait_ge(stats_ok, TILES)
            act.wait_ge(consts, 1)
            nc.scalar.activation(rstd[:, :], moments[:, :, 1], ACT.Sqrt, bias=eps[:, 0:1]).then_inc(sqrt_ok, 1)
            act.sem_inc(v1_used, 1)
            with act.Fori(0, GROUPS) as g:
                act.wait_ge(tps_ok, g + 1)
                nc.scalar.copy(xT[:, :, :], tps[:, :, :]).then_inc(xT_ok, 1)
                act.wait_ge(v1_ok, g + 1)
                act.sem_inc(act_turn, 1)
                nc.scalar.copy(v1p[:, 0, ds(g * GT, GT), :], v1[:, :, :]).then_inc(hi_ok, 1)
                act.wait_ge(rest_ok, g + 1)
                act.sem_inc(act_turn, 1)
                nc.scalar.copy(v1p[:, 1, ds(g * GT, GT), :], rest[:, :, :]).then_inc(mid_ok, 1)

        @block.tensor
        def _(pe):
            pe.wait_ge(consts, 2)
            pe.wait_ge(w_in, 32)
            pe.sem_inc(vps_free, 1)
            with pe.Fori(0, GROUPS) as g:
                pe.wait_ge(xn_ok, g + 1)
                for u in range(GT):
                    for k in range(2):
                        last = nc.tensor.transpose(tps[:, k, u * P:(u + 1) * P],
                                                   XN[:, u, k * P:(k + 1) * P],
                                                   ident_f[:, :])
                last.then_inc(tps_ok, 1)
                pe.wait_ge(xT_ok, g + 1)
                pe.wait_ge(vps_free, g + 1)
                for u in range(GT):
                    for k in range(2):
                        last = nc.tensor.matmul(vps[:, u, 0:D + DN], xT[:, k, u * P:(u + 1) * P], W[:, k, :],
                                                start=(k == 0), stop=(k == 1))
                last.then_inc(vps_ok, 1)


def graph(nc, allocators, src_cols, dst_cols, dst_chunks, span_lo, span_hi, chunk_min, chunk_max, v1p, sumT, ident_h,
          f32, f16, bf16, i32, ALU, ACT, AX, ds):
    with ExitStack() as ctx:
        sb, pb, sem = allocators(ctx)
        counts = [sb("counts_even", [P, SRC_PAD, BN], f16), sb("counts_odd", [P, SRC_PAD, BN], f16)]
        countsT = sb("countsT", [P, 2, CT * BLOCK], f16)
        src_hot = sb("src_hot", [P, 2, UNIT, P], f16)
        pair_hot = sb("pair_hot", [P, 2, UNIT, WCOL], f16)
        row_code = sb("row_code", [P, CHUNKS_PAD], f32)
        col_code = sb("col_code", [P, CHUNKS_PAD], f32)
        iota_row = sb("iota_row", [P, P], f16)
        iota_col = sb("iota_col", [P, WCOL], f16)
        win_row = sb("win_row", [P, WIN_PAD], f32)
        win_col = sb("win_col", [P, WIN_PAD], f32)
        stage_s = sb("stage_s", [P, BLOCK], f32)
        stage_d = sb("stage_d", [P, BN], f32)
        lo_f = sb("lo_f", [1, WINDOWS], f32)
        hi_f = sb("hi_f", [1, WINDOWS], f32)
        tmp_a = sb("tmp_a", [1, WINDOWS], f32)
        tmp_b = sb("tmp_b", [1, WINDOWS], f32)
        firsts = sb("firsts", [1, WINDOWS], i32)
        units = sb("units", [1, WINDOWS], i32)
        v1_band = sb("v1_band", [P, 2, PARTS, CT * DN], bf16)
        longest = sb("longest", [1, 2], f32)
        longest_i = sb("longest_i", [1, 2], i32)
        zeros = sb("zeros", [P, P], f16)
        win_ps = [pb("win_even", [P, 2, 512], f32), pb("win_odd", [P, 2, 512], f32)]
        turned = pb("turned", [P, 2 * 512], f32)
        dst_ps = pb("dst_ps", [P, 512], f32)
        src_ps = pb("src_ps", [P, 512], f32)

        taken = {i32: 0, f32: 0}

        def take(n, dt):
            taken[dt] += n
            flat = counts[dt == f32][:, :, :].rearrange("p a b -> p (a b)")
            return flat.bitcast(dt)[:, taken[dt] - n:taken[dt]]

        src_i, dst_i, part_a, part_b, dst_by_chunk = (take(CHUNKS_PAD, i32) for _ in range(5))
        win_i, iota_i, after_i = take(WIN_PAD, i32), take(WCOL, i32), take(CHUNKS, i32)
        min_row, max_row, after, before, found = (take(CHUNKS, f32) for _ in range(5))
        dst_f = take(CHUNKS_PAD, f32)
        ends = take(2 * CHUNK_TILES, f32)
        first_node = take(2 * WIN_TILES, f32)
        spans = take(2 * WIN_TILES, f32)

        edges_in, iotas, own, ends_ok, ends_out, rows_in = (sem("edges_in"), sem("iotas"), sem("own"),
                                                           sem("ends_ok"), sem("ends_out"), sem("rows_in"))
        spans_ok, spans_out, spans_in = sem("spans_ok"), sem("spans_out"), sem("spans_in")
        ranges_ok, longest_ok, ranges_used = sem("ranges_ok"), sem("longest_ok"), sem("ranges_used")
        hot_ok, hot_free, win_ok, win_free = sem("hot_ok"), sem("hot_free"), sem("win_ok"), sem("win_free")
        turned_ok, turned_free = sem("turned_ok"), sem("turned_free")
        src_ok, src_staged, src_added = sem("src_ok"), sem("src_staged"), sem("src_added")
        dst_ok, dst_staged, dst_added, zeroed = sem("dst_ok"), sem("dst_staged"), sem("dst_added"), sem("zeroed")
        band_ok, band_used = sem("band_ok"), sem("band_used")
        pe_turn, act_turn, dve_turn, pool_turn = (sem("g_pe_turn"), sem("g_act_turn"), sem("g_dve_turn"),
                                                  sem("g_pool_turn"))
        block = ctx.enter_context(nc.Block())

        def passes(eng):
            eng.wait_ge(longest_ok, 1)
            n = eng.value_load(longest_i[0:1, 0:1], min_val=1, max_val=CHUNKS)
            return eng.snap((n + (SUB - 1)) // SUB, min_val=1, max_val=CHUNKS // SUB + 1)

        def values(eng, table, w, n, low, high):
            return nc.values_load_multi_w_load_instructions(
                table[0:1, ds(w, n)], engines=[eng.engine], min_val=low, max_val=high,
                skip_runtime_bounds_check_because="DVE bounds them as it makes the table")[1]

        @block.sync
        def _(sp):
            sp.dma_start(dst_by_chunk.rearrange("p (c e) -> p c e", e=P),
                         dst_chunks.rearrange("(c p) e -> p c e", p=P)).then_inc(edges_in, 16)
            sp.dma_start(dst_i, dst_cols[:, :]).then_inc(edges_in, 16)
            sp.dma_start(src_i, src_cols[:, :]).then_inc(edges_in, 16)
            sp.wait_ge(ends_ok, 1)
            with nc.allow_non_contiguous_dma(reason="a word per chunk, once"):
                sp.dma_start(chunk_min.rearrange("(c p) -> p c", p=P), ends[:, 0:CHUNK_TILES]).then_inc(ends_out, 16)
                sp.dma_start(chunk_max.rearrange("(c p) -> p c", p=P), ends[:, CHUNK_TILES:]).then_inc(ends_out, 16)
            sp.wait_ge(ends_out, 32)
            sp.dma_start(min_row, chunk_min[0:CHUNKS].rearrange("(a n) -> a n", a=1).to_broadcast([P, CHUNKS])).then_inc(rows_in, 16)
            sp.dma_start(max_row, chunk_max[0:CHUNKS].rearrange("(a n) -> a n", a=1).to_broadcast([P, CHUNKS])).then_inc(rows_in, 16)
            sp.wait_ge(spans_ok, 1)
            with nc.allow_non_contiguous_dma(reason="a word per window, once"):
                sp.dma_start(span_lo.rearrange("(c p) -> p c", p=P), spans[:, 0:WIN_TILES]).then_inc(spans_out, 16)
                sp.dma_start(span_hi.rearrange("(c p) -> p c", p=P), spans[:, WIN_TILES:]).then_inc(spans_out, 16)
            sp.wait_ge(spans_out, 32)
            sp.dma_start(lo_f[:, :], span_lo[0:WINDOWS].rearrange("(a n) -> a n", a=1)).then_inc(spans_in, 16)
            sp.dma_start(hi_f[:, :], span_hi[0:WINDOWS].rearrange("(a n) -> a n", a=1)).then_inc(spans_in, 16)

        @block.gpsimd
        def _(pool):
            pool.memset(zeros[:, :], 0.0).then_inc(zeroed, 1)
            pool.iota(iota_i, [[1, WCOL]], base=0, channel_multiplier=0).then_inc(iotas, 1)
            pool.iota(win_i, [[1, WIN_PAD]], base=0, channel_multiplier=0).then_inc(iotas, 1)
            pool.iota(after_i, [[1, CHUNKS]], base=1, channel_multiplier=0).then_inc(iotas, 1)
            pool.iota(part_a[:, 0:WIN_TILES], [[P * WIN, WIN_TILES]], base=0, channel_multiplier=WIN).then_inc(iotas, 1)
            pool.memset(sumT[:, :], 0.0).then_inc(src_added, 1)
            pool.memset(stage_d[:, :], 0.0).then_inc(dst_added, 1)
            n_pass = passes(pool)
            with pool.Fori(0, n_pass) as r:
                pool.wait_ge(band_used, r * BANDS + 2)
                pool.sem_inc(pool_turn, 1)
                with pool.Fori(0, BANDS) as g:
                    band = pool.snap(r * BANDS + g)
                    pool.wait_ge(band_used, band + 1)
                    pool.sem_inc(pool_turn, 1)
                    nc.gpsimd.tensor_copy(v1_band[:, ds(g % 2, 1), :, :].rearrange("p a b n -> p (a b) n"),
                                          v1p[:, :, ds(g * CT, CT), :].rearrange("p b t n -> p b (t n)")).then_inc(band_ok, 1)

                    def add_sources(k):
                        pool.wait_ge(src_staged, band * BLOCKS + (k + 2))
                        pool.wait_ge(src_added, band * BLOCKS + (k + 1))
                        pool.wait_ge(dst_added, band + 1)
                        pool.sem_inc(pool_turn, 1)
                        v = sumT[:, ds(k * BLOCK, BLOCK)]
                        pool.tensor_tensor(v, v, stage_s[:, :], ALU.add).then_inc(src_added, 1)

                    with pool.Fori(0, WPB) as k:
                        add_sources(k)
                    pool.wait_ge(dst_staged, band + 2)
                    pool.wait_ge(src_added, band * BLOCKS + BLOCKS)
                    pool.sem_inc(pool_turn, 1)
                    v = sumT[:, ds(g * BN, BN)]
                    pool.tensor_tensor(v, v, stage_d[:, :], ALU.add).then_inc(dst_added, 1)
                    pool.wait_ge(dst_added, band + 2)
                    pool.sem_inc(pool_turn, 1)
                    pool.wait_ge(src_staged, band * BLOCKS + (BLOCKS + 1))
                    pool.sem_inc(pool_turn, 1)
                    v = sumT[:, (BLOCKS - 1) * BLOCK:BLOCKS * BLOCK]
                    pool.tensor_tensor(v, v, stage_s[:, :], ALU.add).then_inc(src_added, 1)

        @block.vector
        def _(dve):
            step = Steps(dve, own)

            def then(ins):
                step.done(ins)
                step.wait()

            dve.wait_ge(iotas, 4)
            dve.wait_ge(edges_in, 48)
            nc.vector.tensor_copy(iota_row[:, :], iota_i[:, 0:P])
            nc.vector.tensor_copy(iota_col[:, :], iota_i)
            nc.vector.tensor_scalar(win_row[:, :], win_i, -float(P), None, ALU.mult)
            nc.vector.tensor_scalar(win_col[:, :], win_i, -float(WIN), None, ALU.mult)
            nc.vector.tensor_scalar(first_node[:, 0:WIN_TILES], part_a[:, 0:WIN_TILES], 1.0, None, ALU.mult)
            nc.vector.tensor_scalar(first_node[:, WIN_TILES:], part_a[:, 0:WIN_TILES], float(WIN), None, ALU.add)
            nc.vector.tensor_copy(after, after_i)
            then(nc.vector.tensor_copy(dst_f, dst_by_chunk))
            by_chunk = dst_f.rearrange("p (c e) -> p c e", e=P)
            nc.vector.tensor_reduce(out=ends[:, 0:CHUNK_TILES], in_=by_chunk, op=ALU.min, axis=AX.X)
            nc.vector.tensor_reduce(out=ends[:, CHUNK_TILES:], in_=by_chunk, op=ALU.max, axis=AX.X).then_inc(ends_ok, 1)
            nc.vector.tensor_scalar(before, after, -1.0, float(CHUNKS + 1), ALU.mult, ALU.add)
            nc.vector.tensor_single_scalar(part_a, src_i, P - 1, ALU.bitwise_and)
            then(nc.vector.tensor_single_scalar(part_b, dst_i, 4, ALU.arith_shift_right))
            then(nc.vector.scalar_tensor_tensor(row_code[:, :], part_b, float(P), part_a, ALU.mult, ALU.add))
            then(nc.vector.tensor_single_scalar(part_a, src_i, 7, ALU.arith_shift_right))
            then(nc.vector.scalar_tensor_tensor(col_code[:, :], part_a, float(WIN), dst_i, ALU.mult, ALU.add))
            dve.wait_ge(rows_in, 32)
            for q in range(WIN_TILES):
                then(nc.vector.scalar_tensor_tensor(found, max_row, first_node[:, q:q + 1], before, ALU.is_ge, ALU.mult))
                then(nc.vector.tensor_reduce(out=spans[:, q:q + 1], in_=found, op=ALU.max, axis=AX.X))
                then(nc.vector.scalar_tensor_tensor(found, min_row, first_node[:, WIN_TILES + q:WIN_TILES + q + 1],
                                                    after, ALU.is_lt, ALU.mult))
                then(nc.vector.tensor_reduce(out=spans[:, WIN_TILES + q:WIN_TILES + q + 1], in_=found,
                                             op=ALU.max, axis=AX.X))
            nc.vector.tensor_scalar(spans[:, 0:WIN_TILES], spans[:, 0:WIN_TILES], -1.0, float(CHUNKS),
                                    ALU.mult, ALU.add).then_inc(spans_ok, 1)
            dve.wait_ge(spans_in, 32)
            then(nc.vector.tensor_tensor(tmp_a[:, :], hi_f[:, :], lo_f[:, :], ALU.subtract))
            then(nc.vector.tensor_reduce(out=longest[:, 0:1], in_=tmp_a[:, :], op=ALU.max, axis=AX.X))
            then(nc.vector.tensor_scalar(longest[:, 1:2], longest[:, 0:1], 1.0, None, ALU.max))
            nc.vector.tensor_copy(longest_i[:, 0:1], longest[:, 1:2]).then_inc(longest_ok, 1)
            before_passes = step.n
            n_pass = passes(dve)
            made = dve.alloc_register("units_made")
            need = dve.alloc_register("units_needed")
            marks = [dve.alloc_register("units_even"), dve.alloc_register("units_odd")]
            dve.reg_mov(made, 0)
            for m in marks:
                dve.reg_mov(m, 0)
            with dve.Fori(0, n_pass) as r:
                step.at(r * 17 + before_passes)
                dve.wait_ge(ranges_used, r + 1)
                then(nc.vector.tensor_tensor(tmp_a[:, :], lo_f[:, :], hi_f[:, :], ALU.is_lt))
                then(nc.vector.tensor_scalar(tmp_b[:, :], lo_f[:, :], float(-CHUNKS), None, ALU.add))
                then(nc.vector.tensor_tensor(tmp_b[:, :], tmp_b[:, :], tmp_a[:, :], ALU.mult))
                then(nc.vector.tensor_scalar(firsts[:, :], tmp_b[:, :], float(CHUNKS), None, ALU.add))
                then(nc.vector.tensor_tensor(tmp_b[:, :], hi_f[:, :], lo_f[:, :], ALU.subtract))
                then(nc.vector.tensor_scalar(lo_f[:, :], lo_f[:, :], float(SUB), None, ALU.add))
                then(nc.vector.tensor_scalar(tmp_a[:, :], tmp_b[:, :], 0.0, 1.0, ALU.mult, ALU.add))
                for n in range(1, SUB // UNIT):
                    then(nc.vector.scalar_tensor_tensor(tmp_a[:, :], tmp_b[:, :], float(n * UNIT), tmp_a[:, :],
                                                        ALU.is_gt, ALU.add))
                then(nc.vector.tensor_copy(units[:, :], tmp_a[:, :]))
                dve.sem_inc(ranges_ok, 1)
                with dve.Fori(0, WINDOWS // LOAD) as half_band:
                    lo = values(dve, firsts, half_band * LOAD, LOAD, 0, CHUNKS)
                    n = values(dve, units, half_band * LOAD, LOAD, 1, SUB // UNIT)
                    for k in range(LOAD):
                        s = k % 2
                        w = dve.snap(half_band * LOAD + k, min_val=0, max_val=WINDOWS - 1)
                        dve.reg_mov(need, marks[s])
                        with dve.Fori(0, n[k]) as unit:
                            c = dve.snap(lo[k] + unit * UNIT, min_val=0, max_val=CHUNKS + SUB)
                            dve.wait_ge(hot_free, dve.snap(need) + 1)
                            dve.sem_inc(dve_turn, 1)
                            for u in range(UNIT):
                                nc.vector.tensor_scalar(src_hot[:, s, u, :], iota_row[:, :], row_code[:, ds(c + u, 1)],
                                                        win_row[:, ds(w, 1)], ALU.subtract, ALU.is_equal)
                                last = nc.vector.tensor_scalar(pair_hot[:, s, u, :], iota_col[:, :],
                                                               col_code[:, ds(c + u, 1)], win_col[:, ds(w, 1)],
                                                               ALU.subtract, ALU.is_equal)
                            last.then_inc(hot_ok, 1)
                            dve.reg_add(made, made, 1)
                            dve.reg_mov(need, made)
                        dve.reg_mov(marks[s], made)

        @block.scalar
        def _(act):
            act.sem_inc(win_free, 2)
            act.sem_inc(turned_free, 1)
            act.sem_inc(src_staged, 1)
            act.sem_inc(dst_staged, 1)
            n_pass = passes(act)

            def window(built, k, s, buf):
                act.wait_ge(win_ok, built * WPB + (k + 1))
                act.sem_inc(act_turn, 1)
                nc.scalar.copy(counts[buf][:, :, ds(k * WIN, WIN)].rearrange("p (b h) w -> p b h w", b=2),
                               win_ps[s][:, :, 0:HALF].rearrange("p b (h w) -> p b h w", w=WIN)).then_inc(win_free, 1)

            def turned_copy(band, k, s):
                act.wait_ge(turned_ok, band * BLOCKS + (k + 1))
                nc.scalar.copy(countsT[:, s, :], turned[:, 0:CT * BLOCK]).then_inc(turned_free, 1)

            def sources(band, k):
                act.wait_ge(src_ok, band * BLOCKS + (k + 1))
                act.wait_ge(src_added, band * BLOCKS + (k + 1))
                nc.scalar.copy(stage_s[:, :], src_ps[:, 0:BLOCK]).then_inc(src_staged, 1)

            def multiply_step(band, k, s):
                turned_copy(band, k + 1, 1 - s)
                sources(band, k)

            def end_of_band(band):
                act.wait_ge(dst_ok, band + 1)
                act.wait_ge(dst_added, band + 1)
                nc.scalar.copy(stage_d[:, :], dst_ps[:, 0:BN]).then_inc(dst_staged, 1)
                sources(band, BLOCKS - 1)

            with act.Fori(0, n_pass) as r:
                with act.Fori(0, WPB // 2) as q:
                    for s in range(2):
                        window(r * BANDS, q * 2 + s, s, 0)
                with act.Fori(0, BANDS // 2) as i:
                    for odd in range(2):
                        band = act.snap(r * BANDS + i * 2 + odd)
                        turned_copy(band, 0, 0)
                        with act.Fori(0, WPB // 2) as q:
                            for s in range(2):
                                window(band + 1, q * 2 + s, s, 1 - odd)
                                multiply_step(band, q * 2 + s, s)
                        end_of_band(band)
                band = act.snap(r * BANDS + (BANDS - 1))
                turned_copy(band, 0, 0)
                with act.Fori(0, WPB // 2) as q:
                    for s in range(2):
                        multiply_step(band, q * 2 + s, s)
                end_of_band(band)

        @block.tensor
        def _(pe):
            pe.wait_ge(zeroed, 1)
            pe.sem_inc(hot_free, 1)
            pe.sem_inc(ranges_used, 1)
            pe.sem_inc(band_used, 2)
            n_pass = passes(pe)
            seen = pe.alloc_register("units_seen")
            pe.reg_mov(seen, 0)

            def window(built, k, n):
                ps = win_ps[k % 2]
                pe.wait_ge(win_free, built * WPB + (k + 1))
                for b in range(2):
                    nc.tensor.matmul(ps[:, b, HALF:HALF + 1], zeros[:, :], zeros[:, 0:1], start=True, stop=False)
                with pe.Fori(0, n) as _:
                    pe.reg_add(seen, seen, 1)
                    pe.wait_ge(hot_ok, pe.snap(seen))
                    for u in range(UNIT):
                        for b in range(2):
                            last = nc.tensor.matmul(ps[:, b, 0:HALF], src_hot[:, k % 2, u, :],
                                                    pair_hot[:, k % 2, u, b * HALF:(b + 1) * HALF], start=False, stop=False)
                    last.then_inc(hot_free, 1)
                for b in range(2):
                    last = nc.tensor.matmul(ps[:, b, HALF:HALF + 1], zeros[:, :], zeros[:, 0:1], start=False, stop=True)
                last.then_inc(win_ok, 1)

            def turn(k, buf):
                for t in range(CT):
                    for u in range(BT):
                        last = nc.tensor.matmul(turned[:, (t * BT + u) * P:(t * BT + u + 1) * P],
                                                counts[buf][:, k * BT + u, t * P:(t + 1) * P],
                                                ident_h[:, :], start=True, stop=True)
                last.then_inc(turned_ok, 1)

            def to_destinations(k, buf, final=False):
                for u in range(BT):
                    for part in range(PARTS):
                        last = nc.tensor.matmul(dst_ps[:, 0:BN], v1p[:, part, k * BT + u, :], counts[buf][:, k * BT + u, :],
                                                start=(k == 0 and u == 0 and part == 0),
                                                stop=(final and u == BT - 1 and part == PARTS - 1))
                return last

            def to_sources(band, k, buf):
                pe.wait_ge(src_staged, band * BLOCKS + (k + 1))
                for t in range(CT):
                    for part in range(PARTS):
                        last = nc.tensor.matmul(src_ps[:, 0:BLOCK], v1_band[:, buf, part, t * DN:(t + 1) * DN],
                                                countsT[:, k % 2, t * BLOCK:(t + 1) * BLOCK],
                                                start=(t == 0 and part == 0), stop=(t == CT - 1 and part == PARTS - 1))
                return last.then_inc(src_ok, 1)

            def stage(band, buf, built, g_built):
                pe.wait_ge(band_ok, band + 1)
                pe.wait_ge(win_free, band * WPB + (WPB + 2))
                pe.wait_ge(dst_staged, band + 1)
                pe.wait_ge(turned_free, band * BLOCKS + 1)
                turn(0, buf)
                n = None
                for k in range(WPB):
                    if built is not None:
                        if k % LOAD == 0:
                            n = values(pe, units, g_built * WPB + k, LOAD, 1, SUB // UNIT)
                        window(built, k, n[k % LOAD])
                    to_destinations(k, buf)
                    pe.wait_ge(turned_free, band * BLOCKS + (k + 2))
                    turn(k + 1, buf)
                    to_sources(band, k, buf)
                to_destinations(BLOCKS - 1, buf, True).then_inc(dst_ok, 1)
                pe.wait_ge(turned_free, band * BLOCKS + (BLOCKS + 1))
                to_sources(band, BLOCKS - 1, buf)
                pe.sem_inc(band_used, 1)

            with pe.Fori(0, n_pass) as r:
                pe.wait_ge(ranges_ok, r + 1)
                pe.sem_inc(pe_turn, 1)
                for h in range(WPB // LOAD):
                    n = values(pe, units, h * LOAD, LOAD, 1, SUB // UNIT)
                    for k in range(LOAD):
                        window(pe.snap(r * BANDS), h * LOAD + k, n[k])
                with pe.Fori(0, BANDS // 2) as i:
                    for odd in range(2):
                        band = pe.snap(r * BANDS + i * 2 + odd)
                        stage(band, odd, pe.snap(band + 1), pe.snap(i * 2 + (odd + 1)))
                stage(pe.snap(r * BANDS + (BANDS - 1)), 0, None, None)
                pe.sem_inc(ranges_used, 1)


def ffn(nc, allocators, residual, sumT, ident_f, W1, b1, Wg, bg, Wd, bd, out,
        f32, f16, bf16, i32, ALU, ACT, AX, ds):
    with ExitStack() as ctx:
        sb, _, _ = allocators(ctx)
        rows = nc.dram_tensor("rows", [TILES * P, 2 * D], f32, kind="Internal").ap()
        order = nc.dram_tensor("order", [SLOTS, 4], i32, kind="Internal").ap()
        w1 = sb("w1", [P, K1, HID], f32)
        b1c = sb("b1c", [P, KH], f32)
        wd = sb("wd", [P, KH, EXPERTS * D], f32)
        bdr = sb("bdr", [P, EXPERTS * D], f32)
        expert = sb("expert", [P, SLOT_TILES], i32)
        route(nc, allocators, residual, sumT, ident_f, W1, b1, Wg, bg, Wd, bd, rows, order, w1, b1c, wd, bdr, expert,
              f32, i32, ALU, ACT, AX, ds)
        experts(nc, allocators, ident_f, rows, order, w1, b1c, wd, bdr, expert, out,
                f32, i32, ALU, ACT, AX, ds)


def spread(ap, shape):
    return ap.unsqueeze(2).to_broadcast(shape)


def route(nc, allocators, residual, sumT, ident_f, W1, b1, Wg, bg, Wd, bd, rows, order, w1, b1c, wd, bdr, expert,
          f32, i32, ALU, ACT, AX, ds):
    with ExitStack() as ctx:
        sb, pb, sem = allocators(ctx)
        X = sb("rX", [P, TILES, D], f32)
        XN = sb("rXN", [P, GT, D], f32)
        nbT = sb("nbT", [P, GN], f32)
        wg = sb("wg", [P, KH, EXPERTS], f32)
        bgr = sb("bgr", [P, EXPERTS], f32)
        eps = sb("r_eps", [P, 1], f32)
        stats = sb("r_stats", [P, TILES, 6], f32)
        mv = sb("r_mv", [P, TILES, 2], f32)
        rstd = sb("r_rstd", [P, TILES], f32)
        xT = sb("r_xT", [P, K1, GN], f32)
        H = sb("r_H", [P, KH, GN], f32)
        logits = sb("logits", [P, TILES, EXPERTS], f32)
        hflat = H[:, :, :].rearrange("p a b -> p (a b)")
        taken = [0]

        def take(*dims):
            n = dims[0] * (dims[1] if len(dims) > 1 else 1)
            taken[0] += n
            v = hflat[:, taken[0] - n:taken[0]]
            return v.rearrange("p (a b) -> p a b", b=dims[1]) if len(dims) > 1 else v

        TE = (TILES, EXPERTS)
        expo, prob, cand, sel, place = take(*TE), take(*TE), take(*TE), take(*TE), take(*TE)
        scan = [take(*TE), take(*TE)]
        per_tile = take(SLOT_TILES, EXPERTS)
        top, weight, tok, valid, pos = (take(TILES) for _ in range(5))
        tiles_of, ends, ends_b, base = (take(EXPERTS) for _ in range(4))
        tiles_i = take(EXPERTS).bitcast(i32)
        expert_f = take(SLOT_TILES)
        rank = sb("rank", [P, EXPERTS], f32)
        slot_no = sb("slot_no", [P, SLOT_TILES], f32)
        earlier = sb("earlier", [P, P], f32)
        ones = sb("ones", [P, P], f32)
        ints = sb("ints", [P, TILES + SLOT_TILES + EXPERTS], i32)
        pos_i = sb("pos_i", [P, TILES], i32)
        entry = sb("entry", [P, TILES, 4], i32)
        blank = sb("blank", [P, SLOT_TILES, 4], i32)
        nb = pb("nb", [P, GN], f32)
        up = pb("r_up", [P, 2, 512], f32)
        tps = pb("r_tps", [P, K1, GN], f32)
        gate = pb("gate", [P, GT, EXPERTS], f32)
        before_ps = pb("before_ps", [P, 512], f32)
        total_ps = pb("total_ps", [P, 512], f32)

        x_in, w_in, wd_in, consts, own = sem("r_x_in"), sem("r_w_in"), sem("wd_in"), sem("r_consts"), sem("r_own")
        nb_in, nb_free, nb_ok, nb_used = sem("nb_in"), sem("nb_free"), sem("nb_ok"), sem("nb_used")
        var_ok, std_ok, xn_ok, rows_out = sem("var_ok"), sem("std_ok"), sem("r_xn_ok"), sem("rows_out")
        tps_ok, xT_ok, up_ok, h_ok, gate_ok, gate_used = (sem("r_tps_ok"), sem("r_xT_ok"), sem("up_ok"), sem("h_ok"),
                                                          sem("gate_ok"), sem("gate_used"))
        shift_ok, exp_ok, sel_ok, ranks_ok, pos_ok = (sem("shift_ok"), sem("exp_ok"), sem("sel_ok"), sem("ranks_ok"),
                                                      sem("pos_ok"))
        blank_ok, blank_out, entries_out = sem("blank_ok"), sem("blank_out"), sem("entries_out")
        pe_turn, act_turn, dve_turn, pool_turn, pool_own = (sem("r_pe_turn"), sem("r_act_turn"), sem("r_dve_turn"),
                                                            sem("r_pool_turn"), sem("r_pool_own"))
        block = ctx.enter_context(nc.Block())
        res_t = residual.rearrange("(t p) d -> p t d", p=P)
        rows_t = rows.rearrange("(t p) d -> p t d", p=P)

        def row(a, n):
            return a.rearrange("(a n) -> a n", a=1).to_broadcast([P, n])

        @block.sync
        def _(sp):
            sp.dma_start(X[:, 0:GT, :], res_t[:, 0:GT, :]).then_inc(x_in, 16)
            with sp.Fori(1, GROUPS) as g:
                sp.wait_ge(x_in, g * 16)
                sp.dma_start(X[:, ds(g * GT, GT), :], res_t[:, ds(g * GT, GT), :]).then_inc(x_in, 16)
            sp.wait_ge(blank_ok, 2)
            sp.dma_start(order.rearrange("(t p) d -> p t d", p=P), blank[:, :, :]).then_inc(blank_out, 16)
            with sp.Fori(0, GROUPS) as g:
                sp.wait_ge(xn_ok, g + 1)
                sp.dma_start(rows_t[:, ds(g * GT, GT), 0:D], X[:, ds(g * GT, GT), :]).then_inc(rows_out, 16)
                sp.dma_start(rows_t[:, ds(g * GT, GT), D:2 * D], XN[:, :, :]).then_inc(rows_out, 16)
            sp.wait_ge(rows_out, GROUPS * 32)

        @block.gpsimd
        def _(pool):
            pool.memset(eps[:, :], EPS).then_inc(consts, 1)
            pool.memset(ones[:, :], 1.0).then_inc(pool_own, 1)
            pool.memset(blank[:, :, :], 0).then_inc(pool_own, 1)
            pool.wait_ge(pool_own, 2)
            pool.affine_select(out=earlier[:, :], in_=ones[:, :], compare_op=ALU.is_gt, fill=0.0,
                               base=0, pattern=[[1, P]], channel_multiplier=-1).then_inc(consts, 1)
            pool.iota(blank[:, :, 0], [[0, SLOT_TILES]], base=NODES, channel_multiplier=0).then_inc(blank_ok, 1)
            pool.iota(blank[:, :, 1], [[0, SLOT_TILES]], base=NOWHERE, channel_multiplier=0).then_inc(blank_ok, 1)
            pool.iota(ints[:, 0:TILES], [[P, TILES]], base=0, channel_multiplier=1).then_inc(pool_own, 1)
            pool.iota(ints[:, TILES:TILES + SLOT_TILES], [[1, SLOT_TILES]], base=0, channel_multiplier=0).then_inc(pool_own, 1)
            pool.iota(ints[:, TILES + SLOT_TILES:], [[-1, EXPERTS]], base=EXPERTS, channel_multiplier=0).then_inc(pool_own, 1)
            pool.wait_ge(pool_own, 5)
            pool.tensor_copy(slot_no[:, :], ints[:, TILES:TILES + SLOT_TILES]).then_inc(consts, 1)
            pool.tensor_copy(rank[:, :], ints[:, TILES + SLOT_TILES:]).then_inc(consts, 1)
            pool.memset(entry[:, :, 3], 0).then_inc(pool_own, 1)
            pool.tensor_copy(entry[:, :, 0], ints[:, 0:TILES]).then_inc(pool_own, 1)
            pool.tensor_copy(entry[:, :, 1], ints[:, 0:TILES]).then_inc(pool_own, 1)
            with pool.Fori(0, GROUPS) as g:
                pool.wait_ge(nb_free, g + 1)
                pool.sem_inc(pool_turn, 1)
                pool.tensor_copy(nbT[:, :], sumT[:, ds(g * GN, GN)]).then_inc(nb_in, 1)
            pool.wait_ge(blank_out, 16)
            pool.wait_ge(pool_own, 8)
            pool.wait_ge(pos_ok, 2)
            for t in range(TILES):
                pool.indirect_dma_start(order[:, :], bass.IndirectOffsetOnAxis(pos_i[:, t:t + 1], 0), entry[:, t, :], None,
                                        bounds_check=SLOTS - 1, oob_is_err=False).then_inc(entries_out, 16)
            pool.wait_ge(entries_out, TILES * 16)

        @block.vector
        def _(dve):
            step = Steps(dve, own)

            def then(ins):
                step.done(ins)
                step.wait()

            with dve.Fori(0, GROUPS) as g:
                step.at(g * 5)
                dve.wait_ge(x_in, g * 16 + 16)
                dve.wait_ge(nb_ok, g + 1)
                x = X[:, ds(g * GT, GT), 0:DN]
                then(nc.vector.tensor_tensor(x, x, nb[:, :].rearrange("p (t n) -> p t n", n=DN), ALU.add))
                dve.sem_inc(nb_used, 1)
                for t in range(GT):
                    step.done(nc.vector.bn_stats(flat2(stats[:, ds(g * GT + t, 1), :]), flat2(X[:, ds(g * GT + t, 1), :])))
                assert step.n == 5
            step.at(GROUPS * 5)
            step.wait()
            for t in range(TILES):
                nc.vector.bn_aggr(mv[:, t, :], stats[:, t, :]).then_inc(var_ok, 1)
            dve.wait_ge(std_ok, 1)
            then(nc.vector.reciprocal(rstd[:, :], rstd[:, :]))
            dve.wait_ge(w_in, 16 * 4)

            def normalise(g):
                for u in range(GT):
                    last = nc.vector.tensor_scalar(XN[:, u, :], flat2(X[:, ds(g * GT + u, 1), :]),
                                                   flat2(mv[:, ds(g * GT + u, 1), 0:1]), rstd[:, ds(g * GT + u, 1)],
                                                   ALU.subtract, ALU.mult)
                last.then_inc(xn_ok, 1)

            def add_bias(g):
                dve.wait_ge(gate_ok, g + 1)
                dve.sem_inc(dve_turn, 1)
                nc.vector.tensor_tensor(logits[:, ds(g * GT, GT), :], gate[:, :, :],
                                        bgr[:, :].unsqueeze(1).to_broadcast([P, GT, EXPERTS]), ALU.add).then_inc(gate_used, 1)

            normalise(0)
            with dve.Fori(0, GROUPS - 1) as g:
                dve.wait_ge(tps_ok, g + 1)
                dve.wait_ge(rows_out, g * 32 + 32)
                dve.sem_inc(dve_turn, 1)
                normalise(g + 1)
                add_bias(g)
            add_bias(GROUPS - 1)
            dve.wait_ge(gate_used, GROUPS + 1)
            shape = [P, TILES, EXPERTS]
            then(nc.vector.tensor_reduce(out=top, in_=logits[:, :, :], op=ALU.max, axis=AX.X))
            nc.vector.tensor_tensor(cand, logits[:, :, :], spread(top, shape), ALU.subtract).then_inc(shift_ok, 1)
            dve.wait_ge(exp_ok, 1)
            then(nc.vector.tensor_reduce(out=top, in_=expo, op=ALU.add, axis=AX.X))
            then(nc.vector.reciprocal(top, top))
            then(nc.vector.tensor_tensor(prob, expo, spread(top, shape), ALU.mult))
            dve.wait_ge(consts, 4)
            dve.wait_ge(pool_own, 8)
            then(nc.vector.tensor_reduce(out=weight, in_=prob, op=ALU.max, axis=AX.X))
            then(nc.vector.tensor_tensor(cand, prob, spread(weight, shape), ALU.is_equal))
            then(nc.vector.tensor_tensor(cand, cand, rank[:, :].unsqueeze(1).to_broadcast(shape), ALU.mult))
            then(nc.vector.tensor_reduce(out=top, in_=cand, op=ALU.max, axis=AX.X))
            step.done(nc.vector.tensor_tensor(sel, cand, spread(top, shape), ALU.is_equal))
            then(nc.vector.tensor_scalar(valid, ints[:, 0:TILES], float(NODES), None, ALU.is_lt))
            nc.vector.tensor_copy(entry[:, :, 2], weight.bitcast(i32)).then_inc(pos_ok, 1)
            then(nc.vector.tensor_tensor(sel, sel, spread(valid, shape), ALU.mult))
            dve.sem_inc(sel_ok, 1)
            dve.wait_ge(ranks_ok, 1)
            total = total_ps[:, 0:TILES * EXPERTS].rearrange("p (t e) -> p t e", e=EXPERTS)
            before = before_ps[:, 0:TILES * EXPERTS].rearrange("p (t e) -> p t e", e=EXPERTS)
            then(nc.vector.tensor_copy(scan[0], total))
            a, b, far = 0, 1, 1
            while far < TILES:
                step.done(nc.vector.tensor_copy(scan[b][:, 0:far, :], scan[a][:, 0:far, :]))
                then(nc.vector.tensor_tensor(scan[b][:, far:, :], scan[a][:, far:, :], scan[a][:, 0:TILES - far, :], ALU.add))
                a, b, far = b, a, 2 * far
            then(nc.vector.tensor_scalar(tiles_of, scan[a][:, TILES - 1, :], float(P - 1), None, ALU.add))
            then(nc.vector.tensor_copy(tiles_i, tiles_of))
            then(nc.vector.tensor_single_scalar(tiles_i, tiles_i, 7, ALU.arith_shift_right))
            then(nc.vector.tensor_copy(tiles_of, tiles_i))
            then(nc.vector.tensor_copy(ends, tiles_of))
            e0, e1, far = ends, ends_b, 1
            while far < EXPERTS:
                step.done(nc.vector.tensor_copy(e1[:, 0:far], e0[:, 0:far]))
                then(nc.vector.tensor_tensor(e1[:, far:], e0[:, far:], e0[:, 0:EXPERTS - far], ALU.add))
                e0, e1, far = e1, e0, 2 * far
            then(nc.vector.tensor_tensor(base, e0, tiles_of, ALU.subtract))
            then(nc.vector.tensor_scalar(base, base, float(P), None, ALU.mult))
            then(nc.vector.tensor_tensor(place, scan[a], total, ALU.subtract))
            then(nc.vector.tensor_tensor(place, place, before, ALU.add))
            then(nc.vector.tensor_tensor(place, place, base.unsqueeze(1).to_broadcast(shape), ALU.add))
            then(nc.vector.tensor_tensor(place, place, sel, ALU.mult))
            step.done(nc.vector.tensor_reduce(out=pos, in_=place, op=ALU.add, axis=AX.X))
            then(nc.vector.tensor_scalar(valid, valid, -float(NOWHERE), float(NOWHERE), ALU.mult, ALU.add))
            then(nc.vector.tensor_tensor(pos, pos, valid, ALU.add))
            nc.vector.tensor_copy(pos_i[:, :], pos).then_inc(pos_ok, 1)
            eshape = [P, SLOT_TILES, EXPERTS]
            then(nc.vector.tensor_tensor(per_tile, spread(slot_no[:, :], eshape), e0.unsqueeze(1).to_broadcast(eshape), ALU.is_ge))
            then(nc.vector.tensor_reduce(out=expert_f, in_=per_tile, op=ALU.add, axis=AX.X))
            then(nc.vector.tensor_scalar(expert_f, expert_f, float(EXPERTS - 1), None, ALU.min))
            then(nc.vector.tensor_copy(expert[:, :], expert_f))

        @block.scalar
        def _(act):
            act.dma_start(w1[:, :, :], W1.rearrange("(k p) n -> p k n", p=P)).then_inc(w_in, 16)
            with nc.allow_non_contiguous_dma(reason="a word per hidden feature, once"):
                act.dma_start(b1c[:, :], b1.rearrange("(k p) -> p k", p=P)).then_inc(w_in, 16)
            act.dma_start(wg[:, :, :], Wg.rearrange("(k p) n -> p k n", p=P)).then_inc(w_in, 16)
            act.dma_start(bgr[:, :], row(bg, EXPERTS)).then_inc(w_in, 16)
            act.dma_start(bdr[:, :], row(bd.rearrange("e d -> (e d)"), EXPERTS * D)).then_inc(wd_in, 16)
            for e in range(EXPERTS):
                act.dma_start(wd[:, :, e * D:(e + 1) * D], Wd[e, :, :].rearrange("(k p) n -> p k n", p=P)).then_inc(wd_in, 16)
            act.wait_ge(consts, 1)
            act.wait_ge(var_ok, TILES)
            nc.scalar.activation(rstd[:, :], mv[:, :, 1], ACT.Sqrt, bias=eps[:, 0:1]).then_inc(std_ok, 1)
            act.wait_ge(w_in, 16 * 4)
            with act.Fori(0, GROUPS) as g:
                act.wait_ge(tps_ok, g + 1)
                nc.scalar.copy(xT[:, :, :], tps[:, :, :]).then_inc(xT_ok, 1)
                for j in range(KH):
                    act.wait_ge(up_ok, g * KH + (j + 1))
                    nc.scalar.activation(H[:, j, :], up[:, j % 2, :], ACT.Gelu, bias=b1c[:, j:j + 1]).then_inc(h_ok, 1)
            act.wait_ge(gate_ok, GROUPS)
            act.wait_ge(shift_ok, 1)
            nc.scalar.activation(expo, cand, ACT.Exp).then_inc(exp_ok, 1)
            act.wait_ge(wd_in, 16 * (EXPERTS + 1))

        @block.tensor
        def _(pe):
            pe.sem_inc(nb_free, 1)
            with pe.Fori(0, GROUPS) as g:
                pe.wait_ge(nb_in, g + 1)
                for t in range(GT):
                    last = nc.tensor.transpose(nb[:, t * P:(t + 1) * P], nbT[:, t * P:(t + 1) * P], ident_f[:, :])
                last.then_inc(nb_ok, 1)
                pe.wait_ge(nb_used, g + 1)
                pe.sem_inc(nb_free, 1)
            pe.wait_ge(w_in, 16 * 4)
            pe.sem_inc(gate_used, 1)

            def turn(g):
                pe.wait_ge(xn_ok, g + 1)
                for t in range(GT):
                    for k in range(K1):
                        last = nc.tensor.transpose(tps[:, k, t * P:(t + 1) * P], XN[:, t, k * P:(k + 1) * P], ident_f[:, :])
                last.then_inc(tps_ok, 1)

            def hidden(g):
                pe.wait_ge(xT_ok, g + 1)
                for j in range(KH):
                    pe.wait_ge(h_ok, g * KH + (j - 1 + 2))
                    for k in range(K1):
                        last = nc.tensor.matmul(up[:, j % 2, :], w1[:, k, j * P:(j + 1) * P], xT[:, k, :],
                                                start=(k == 0), stop=(k == K1 - 1))
                    last.then_inc(up_ok, 1)

            def logit(g):
                pe.wait_ge(h_ok, g * KH + (KH + 2))
                pe.wait_ge(gate_used, g + 1)
                for t in range(GT):
                    for j in range(KH):
                        last = nc.tensor.matmul(gate[:, t, :], H[:, j, t * P:(t + 1) * P], wg[:, j, :],
                                                start=(j == 0), stop=(j == KH - 1))
                last.then_inc(gate_ok, 1)

            pe.sem_inc(h_ok, 2)
            turn(0)
            with pe.Fori(0, GROUPS - 1) as g:
                hidden(g)
                turn(g + 1)
                logit(g)
            hidden(GROUPS - 1)
            logit(GROUPS - 1)
            pe.wait_ge(sel_ok, 1)
            pe.wait_ge(consts, 4)
            flat_sel = sel.rearrange("p t e -> p (t e)")
            nc.tensor.matmul(before_ps[:, 0:TILES * EXPERTS], earlier[:, :], flat_sel, start=True, stop=True)
            nc.tensor.matmul(total_ps[:, 0:TILES * EXPERTS], ones[:, :], flat_sel, start=True, stop=True).then_inc(ranks_ok, 1)


def experts(nc, allocators, ident_f, rows, order, w1, b1c, wd, bdr, expert, out,
            f32, i32, ALU, ACT, AX, ds):
    with ExitStack() as ctx:
        sb, pb, sem = allocators(ctx)
        R = sb("R", [P, 2, GT, 2 * D], f32)
        who = sb("who", [P, SLOT_TILES, 4], i32)
        from_row = sb("from_row", [P, 2, GT], i32)
        to_row = sb("to_row", [P, 2, GT], i32)
        xT = sb("e_xT", [P, K1, GN], f32)
        H = sb("e_H", [P, KH, GN], f32)
        Y = sb("e_Y", [P, 2, GT, D], f32)
        up = pb("e_up", [P, 2, 512], f32)
        tps = pb("e_tps", [P, K1, GN], f32)
        down = pb("down", [P, 2, 512], f32)

        who_in, idx_ok = sem("who_in"), sem("idx_ok")
        row_in = [sem("row_in0"), sem("row_in1")]
        row_out = [sem("row_out0"), sem("row_out1")]
        tps_ok, xT_ok, up_ok, h_ok = sem("e_tps_ok"), sem("e_xT_ok"), sem("e_up_ok"), sem("e_h_ok")
        down_ok, down_used, y_ok, biased = sem("down_ok"), sem("down_used"), sem("y_ok"), sem("biased")
        pe_turn, dve_turn, pool_turn = sem("e_pe_turn"), sem("e_dve_turn"), sem("e_pool_turn")
        block = ctx.enter_context(nc.Block())
        PAIRS_E = SLOT_TILES // GT // 2

        @block.sync
        def _(sp):
            sp.dma_start(who[:, :, :], order.rearrange("(t p) d -> p t d", p=P)).then_inc(who_in, 16)

        @block.gpsimd
        def _(pool):
            def gather(i, s):
                nc.gpsimd.tensor_copy(from_row[:, s, :], who[:, ds(i * (2 * GT) + s * GT, GT), 0]).then_inc(idx_ok, 1)
                nc.gpsimd.tensor_copy(to_row[:, s, :], who[:, ds(i * (2 * GT) + s * GT, GT), 1]).then_inc(idx_ok, 1)
                pool.wait_ge(idx_ok, i * 4 + (2 * s + 2))
                pool.sem_inc(pool_turn, 1)
                for u in range(GT):
                    pool.indirect_dma_start(R[:, s, u, :], None, rows[:, :],
                                            bass.IndirectOffsetOnAxis(from_row[:, s, u:u + 1], 0)).then_inc(row_in[s], 16)

            def scatter(i, s):
                pool.wait_ge(y_ok, i * (2 * GT) + (s + 1) * GT)
                pool.sem_inc(pool_turn, 1)
                for u in range(GT):
                    pool.indirect_dma_start(out[:, :], bass.IndirectOffsetOnAxis(to_row[:, s, u:u + 1], 0),
                                            Y[:, s, u, :], None, bounds_check=NODES - 1,
                                            oob_is_err=False).then_inc(row_out[s], 16)

            def written(i, s):
                pool.wait_ge(row_out[s], i * (16 * GT) + 16 * GT)
                pool.sem_inc(pool_turn, 1)

            pool.wait_ge(who_in, 16)
            gather(0, 0)
            with pool.Fori(0, PAIRS_E - 1) as i:
                gather(i, 1)
                scatter(i, 0)
                written(i, 0)
                gather(i + 1, 0)
                scatter(i, 1)
                written(i, 1)
            gather(PAIRS_E - 1, 1)
            scatter(PAIRS_E - 1, 0)
            scatter(PAIRS_E - 1, 1)
            written(PAIRS_E - 1, 0)
            written(PAIRS_E - 1, 1)

        @block.vector
        def _(dve):
            dve.wait_ge(who_in, 16)
            with dve.Fori(0, PAIRS_E) as i:
                for s in range(2):
                    dve.wait_ge(row_in[s], i * (16 * GT) + 16 * GT)
                    for u in range(GT):
                        n = i * (2 * GT) + (s * GT + u)
                        e = dve.value_load(expert[0:1, ds(n, 1)], min_val=0, max_val=EXPERTS - 1)
                        dve.wait_ge(down_ok, n + 1)
                        dve.sem_inc(dve_turn, 1)
                        y = Y[:, s, u, :]
                        nc.vector.tensor_tensor(y, down[:, u % 2, 0:D], bdr[:, ds(e * D, D)], ALU.add).then_inc(down_used, 1)
                        dve.wait_ge(down_used, n + 3)
                        dve.sem_inc(dve_turn, 1)
                        nc.vector.scalar_tensor_tensor(y, y, flat2(who[:, ds(n, 1), 2:3].bitcast(f32)), R[:, s, u, 0:D],
                                                       ALU.mult, ALU.add).then_inc(y_ok, 1)

        @block.scalar
        def _(act):
            with act.Fori(0, 2 * PAIRS_E) as g:
                act.wait_ge(tps_ok, g + 1)
                nc.scalar.copy(xT[:, :, :], tps[:, :, :]).then_inc(xT_ok, 1)
                for j in range(KH):
                    act.wait_ge(up_ok, g * KH + (j + 1))
                    nc.scalar.activation(H[:, j, :], up[:, j % 2, :], ACT.Gelu, bias=b1c[:, j:j + 1]).then_inc(h_ok, 1)

        @block.tensor
        def _(pe):
            def turn(i, s):
                pe.wait_ge(row_in[s], i * (16 * GT) + 16 * GT)
                for t in range(GT):
                    for k in range(K1):
                        last = nc.tensor.transpose(tps[:, k, t * P:(t + 1) * P], R[:, s, t, D + k * P:D + (k + 1) * P], ident_f[:, :])
                last.then_inc(tps_ok, 1)

            def hidden(i, s):
                g = i * 2 + s
                pe.wait_ge(xT_ok, g + 1)
                for j in range(KH):
                    pe.wait_ge(h_ok, g * KH + (j - 1 + 2))
                    for k in range(K1):
                        last = nc.tensor.matmul(up[:, j % 2, :], w1[:, k, j * P:(j + 1) * P], xT[:, k, :],
                                                start=(k == 0), stop=(k == K1 - 1))
                    last.then_inc(up_ok, 1)

            def products(i, s):
                pe.wait_ge(h_ok, (i * 2 + s) * KH + (KH + 2))
                for u in range(GT):
                    n = i * (2 * GT) + (s * GT + u)
                    e = pe.value_load(expert[0:1, ds(n, 1)], min_val=0, max_val=EXPERTS - 1)
                    pe.wait_ge(down_used, n + 1)
                    pe.sem_inc(pe_turn, 1)
                    for j in range(KH):
                        last = nc.tensor.matmul(down[:, u % 2, 0:D], H[:, j, u * P:(u + 1) * P],
                                                wd[:, j, ds(e * D, D)], start=(j == 0), stop=(j == KH - 1))
                    last.then_inc(down_ok, 1)

            pe.sem_inc(h_ok, 2)
            pe.sem_inc(down_used, 2)
            turn(0, 0)
            with pe.Fori(0, PAIRS_E - 1) as i:
                hidden(i, 0)
                turn(i, 1)
                products(i, 0)
                hidden(i, 1)
                turn(i + 1, 0)
                products(i, 1)
            last_i = PAIRS_E - 1
            hidden(last_i, 0)
            turn(last_i, 1)
            products(last_i, 0)
            hidden(last_i, 1)
            products(last_i, 1)


def kernel(**inputs):
    import numpy as np
    import concourse.bacc as bacc
    from concourse.bass_utils import run_bass_kernel_spmd

    a = {n: np.asarray(v) for n, v in inputs.items()}
    rows = TILES * P
    edges = CHUNKS_PAD * P
    x = np.concatenate([a["x"], np.zeros((rows - NODES, D), np.float32)])
    src = np.concatenate([a["src"], np.zeros(edges - EDGES, np.int32)]).reshape(CHUNKS_PAD, P)
    dst = np.concatenate([a["dst"], np.full(edges - EDGES, NO_NODE, np.int32)]).reshape(CHUNKS_PAD, P)
    arrays = {
        "x": x,
        "src_cols": np.ascontiguousarray(src.T),
        "dst_cols": np.ascontiguousarray(dst.T),
        "dst_chunks": dst,
        "w01": np.ascontiguousarray(np.concatenate([a["L0_gnn_w0_w"], a["L0_gnn_w1_w"]]).T),
        "b01": np.concatenate([a["L0_gnn_w0_b"], a["L0_gnn_w1_b"]]),
        "W1": a["L0_ffn_W1"], "b1": a["L0_ffn_b1"], "Wg": a["L0_ffn_Wg"], "bg": a["L0_ffn_bg"],
        "Wd": a["L0_ffn_Wd"], "bd": a["L0_ffn_bd"],
    }
    nc = bacc.Bacc("TRN2", target_bir_lowering=False, num_devices=1)
    args = {n: nc.dram_tensor("in_" + n, v.shape, mybir.dt.from_np(v.dtype), kind="ExternalInput").ap()
            for n, v in arrays.items()}
    out = nc.dram_tensor("out", (NODES, D), mybir.dt.float32, kind="ExternalOutput").ap()
    build(nc, out=out, **args)
    r = run_bass_kernel_spmd(nc, [{"in_" + n: v for n, v in arrays.items()}], core_ids=[0])
    return r.results[0]["out"]
```

```python
import concourse.bass as bass
from concourse import mybir
from contextlib import ExitStack

P = 128
D = 256
DN = 128
HID = 1024
EXPERTS = 8
NODES = 6250
EDGES = 106250
EPS = 1e-5

TILES = 52
GT = 4
GROUPS = TILES // GT
GN = GT * P
SRC_TILES = 49
SRC_PAD = 50
WIN = 8
CT = 3
BANDS = -(-SRC_TILES // CT)
BN = CT * P
PAIR = 2
WPB = BN // WIN
STEPS = WPB // PAIR
WINDOWS = BANDS * WPB
WCOL = SRC_PAD * WIN
BT = 2
BLOCK = BT * P
BLOCKS = SRC_PAD // BT
CHUNKS = -(-EDGES // P)
CHUNK_TILES = -(-CHUNKS // P)
CHUNKS_PAD = CHUNK_TILES * P
WIN_TILES = -(-WINDOWS // P)
WIN_PAD = WIN_TILES * P
NO_NODE = 8192
UNIT = 2
SUB = 14
RANGE_STEPS = 9
LOAD = WPB // 4
PARTS = 2
LARGE = 2.0 ** 14
ONE_OVER = 254 << 23
assert STEPS == BLOCKS - 1 and LOAD % (2 * PAIR) == 0 and BANDS % 2 == 1 and SUB * P <= 2048

K1, KH = D // P, HID // P
AHEAD = 4
SLOT_TILES = (NODES + EXPERTS * (P - 1)) // P
SLOTS = SLOT_TILES * P
NOWHERE = 1 << 16


class Steps:

    def __init__(self, eng, sem):
        self.eng, self.sem, self.base, self.n = eng, sem, 0, 0

    def at(self, base):
        self.base, self.n = base, 0

    def done(self, ins):
        ins.then_inc(self.sem, 1)
        self.n += 1
        return ins

    def wait(self):
        self.eng.wait_ge(self.sem, self.base + self.n)


def build(nc, x, src_cols, dst_cols, dst_chunks, w01, b01, W1, b1, Wg, bg, Wd, bd, out):
    f32, f16, i32 = mybir.dt.float32, mybir.dt.float16, mybir.dt.int32
    ALU, ACT, AX = mybir.AluOpType, mybir.ActivationFunctionType, mybir.AxisListType
    ds = bass.ds

    with ExitStack() as whole:
        def allocators(ctx):
            return (lambda n, s, d: ctx.enter_context(nc.sbuf_tensor(n, s, d)),
                    lambda n, s, d: ctx.enter_context(nc.psum_tensor(n, s, d)),
                    lambda n: ctx.enter_context(nc.semaphore(n)))

        sb, _, sem = allocators(whole)
        residual = nc.dram_tensor("residual", [TILES * P, D], f32, kind="Internal").ap()
        span_lo = nc.dram_tensor("span_lo", [WIN_PAD], f32, kind="Internal").ap()
        span_hi = nc.dram_tensor("span_hi", [WIN_PAD], f32, kind="Internal").ap()
        chunk_min = nc.dram_tensor("chunk_min", [CHUNKS_PAD], f32, kind="Internal").ap()
        chunk_max = nc.dram_tensor("chunk_max", [CHUNKS_PAD], f32, kind="Internal").ap()
        sumT = sb("sumT", [P, TILES * P], f32)
        ident_f = sb("ident_f", [P, P], f32)
        ident_h = sb("ident_h", [P, P], f16)

        with ExitStack() as front:
            sbf, _, _ = allocators(front)
            v1p = sbf("v1p", [P, PARTS, TILES, DN], f16)
            unscale = sbf("unscale", [P, 1], f32)
            tables = dict(
                row_code=sbf("row_code", [P, CHUNKS_PAD], f32), col_code=sbf("col_code", [P, CHUNKS_PAD], f32),
                iota_row=sbf("iota_row", [P, P], f16), iota_col=sbf("iota_col", [P, WCOL], f16),
                win_row=sbf("win_row", [P, WIN_PAD], f32), win_col=sbf("win_col", [P, WIN_PAD], f32),
                lo_f=sbf("lo_f", [1, WINDOWS], f32), hi_f=sbf("hi_f", [1, WINDOWS], f32))
            prepare(nc, allocators, x, w01, b01, residual, v1p, unscale, sumT, ident_f, ident_h,
                    src_cols, dst_cols, dst_chunks, span_lo, span_hi, chunk_min, chunk_max, tables,
                    f32, f16, i32, ALU, ACT, AX, ds)
            graph(nc, allocators, tables, v1p, unscale, sumT, ident_h,
                  f32, f16, i32, ALU, ACT, AX, ds)
        ffn(nc, allocators, residual, sumT, ident_f, W1, b1, Wg, bg, Wd, bd, out,
            f32, f16, i32, ALU, ACT, AX, ds)


def flat2(ap):
    return ap.rearrange("p a d -> p (a d)")


def prepare(nc, allocators, x, w01, b01, residual, v1p, unscale, sumT, ident_f, ident_h,
            src_cols, dst_cols, dst_chunks, span_lo, span_hi, chunk_min, chunk_max, tables,
            f32, f16, i32, ALU, ACT, AX, ds):
    with ExitStack() as ctx:
        sb, pb, sem = allocators(ctx)
        X = sb("X", [P, TILES, D], f32)
        XN = sb("XN", [P, GT, D], f32)
        Y = sb("Y", [P, GT, D], f32)
        W = sb("W", [P, 2, D + DN], f32)
        bias = sb("bias", [P, D + DN], f32)
        stats = sb("stats", [P, GT, 6], f32)
        moments = sb("moments", [P, GT, 2], f32)
        rstd = sb("rstd", [P, GT], f32)
        eps = sb("eps", [P, 1], f32)
        xT = sb("xT", [P, 2, GN], f32)
        v1 = sb("v1", [P, GT, DN], f32)
        ones = sb("sum_ones", [P, P], f32)
        size = sb("size", [P, 2, DN], f32)
        bound = sb("bound", [P, DN], f32)
        power = sb("power", [P, DN], i32)
        recip = sb("recip", [P, DN], i32)
        tps = pb("tps", [P, 2, GN], f32)
        vps = pb("vps", [P, GT, 512], f32)
        sps = pb("sps", [P, 512], f32)

        def take(name, n, dt):
            return sb(name, [P, n], dt)[:, :]

        src_i, dst_i, part_a, part_b, dst_by_chunk = (take(n, CHUNKS_PAD, i32) for n in
                                                      ("src_i", "dst_i", "part_a", "part_b", "dst_by_chunk"))
        win_i, iota_i, after_i = take("win_i", WIN_PAD, i32), take("iota_i", WCOL, i32), take("after_i", CHUNKS, i32)
        min_row, max_row, after, before, found = (take(n, CHUNKS, f32) for n in
                                                  ("min_row", "max_row", "after", "before", "found"))
        dst_f = take("dst_f", CHUNKS_PAD, f32)
        ends = take("ends", 2 * CHUNK_TILES, f32)
        first_node = take("first_node", 2 * WIN_TILES, f32)
        spans = take("spans", 2 * WIN_TILES, f32)
        row_code, col_code, iota_row, iota_col = tables["row_code"], tables["col_code"], tables["iota_row"], tables["iota_col"]
        win_row, win_col, lo_f, hi_f = tables["win_row"], tables["win_col"], tables["lo_f"], tables["hi_f"]

        edges_in, iotas, zero_sums, ends_ok, ends_out, rows_in = (sem("edges_in"), sem("iotas"), sem("zero_sums"),
                                                                 sem("ends_ok"), sem("ends_out"), sem("rows_in"))
        spans_ok, spans_out, spans_in, setup_own = sem("spans_ok"), sem("spans_out"), sem("spans_in"), sem("setup_own")
        x_in, w_in = sem("x_in"), sem("w_in")
        consts, stats_ok, sqrt_ok = sem("consts"), sem("stats_ok"), sem("sqrt_ok")
        stat_own = sem("stat_own")
        xn_ok, tps_ok, xT_ok, vps_ok = sem("xn_ok"), sem("tps_ok"), sem("xT_ok"), sem("vps_ok")
        vps_read, v1_ok, hi_ok, scale_own = sem("vps_read"), sem("v1_ok"), sem("hi_ok"), sem("scale_own")
        size_ok, size_sum, w_ok, unscale_sum = sem("size_ok"), sem("size_sum"), sem("w_ok"), sem("unscale_sum")
        v1_used, y_ok, res_ok, res_out, pool_own = (sem("v1_used"), sem("y_out_ok"), sem("res_ok"), sem("res_out"),
                                                    sem("pool_own"))
        vps_free, dve_turn, act_turn, pool_turn = sem("vps_free"), sem("dve_turn"), sem("act_turn"), sem("pool_turn")
        block = ctx.enter_context(nc.Block())
        x_t = x.rearrange("(t p) d -> p t d", p=P)
        res_t = residual.rearrange("(t p) d -> p t d", p=P)

        @block.sync
        def _(sp):
            sp.dma_start(X[:, 0:GT, :], x_t[:, 0:GT, :]).then_inc(x_in, 16)
            sp.dma_start(dst_by_chunk.rearrange("p (c e) -> p c e", e=P),
                         dst_chunks.rearrange("(c p) e -> p c e", p=P)).then_inc(edges_in, 16)
            sp.dma_start(dst_i, dst_cols[:, :]).then_inc(edges_in, 16)
            sp.dma_start(src_i, src_cols[:, :]).then_inc(edges_in, 16)
            with sp.Fori(1, GROUPS) as g:
                sp.wait_ge(x_in, g * 16)
                sp.dma_start(X[:, ds(g * GT, GT), :], x_t[:, ds(g * GT, GT), :]).then_inc(x_in, 16)
            sp.wait_ge(ends_ok, 1)
            with nc.allow_non_contiguous_dma(reason="a word per chunk, once"):
                sp.dma_start(chunk_min.rearrange("(c p) -> p c", p=P), ends[:, 0:CHUNK_TILES]).then_inc(ends_out, 16)
                sp.dma_start(chunk_max.rearrange("(c p) -> p c", p=P), ends[:, CHUNK_TILES:]).then_inc(ends_out, 16)
            sp.wait_ge(ends_out, 32)
            sp.dma_start(min_row, chunk_min[0:CHUNKS].rearrange("(a n) -> a n", a=1).to_broadcast([P, CHUNKS])).then_inc(rows_in, 16)
            sp.dma_start(max_row, chunk_max[0:CHUNKS].rearrange("(a n) -> a n", a=1).to_broadcast([P, CHUNKS])).then_inc(rows_in, 16)
            with sp.Fori(0, GROUPS) as g:
                sp.wait_ge(res_ok, g + 2)
                sp.dma_start(res_t[:, ds(g * GT, GT), :], X[:, ds(g * GT, GT), :]).then_inc(res_out, 16)
            sp.wait_ge(spans_ok, 1)
            with nc.allow_non_contiguous_dma(reason="a word per window, once"):
                sp.dma_start(span_lo.rearrange("(c p) -> p c", p=P), spans[:, 0:WIN_TILES]).then_inc(spans_out, 16)
                sp.dma_start(span_hi.rearrange("(c p) -> p c", p=P), spans[:, WIN_TILES:]).then_inc(spans_out, 16)
            sp.wait_ge(spans_out, 32)
            sp.dma_start(lo_f[:, :], span_lo[0:WINDOWS].rearrange("(a n) -> a n", a=1)).then_inc(spans_in, 16)
            sp.dma_start(hi_f[:, :], span_hi[0:WINDOWS].rearrange("(a n) -> a n", a=1)).then_inc(spans_in, 16)
            sp.wait_ge(spans_in, 32)
            sp.wait_ge(res_out, GROUPS * 16)

        @block.gpsimd
        def _(pool):
            pool.memset(eps[:, :], EPS).then_inc(consts, 1)
            pool.memset(ones[:, :], 1.0).then_inc(consts, 1)
            pool.memset(ident_f[:, :], 0.0).then_inc(pool_own, 1)
            pool.wait_ge(pool_own, 1)
            pool.affine_select(out=ident_f[:, :], in_=ident_f[:, :], compare_op=ALU.not_equal, fill=1.0,
                               base=0, pattern=[[-1, P]], channel_multiplier=1).then_inc(pool_own, 1)
            pool.wait_ge(pool_own, 2)
            pool.tensor_copy(ident_h[:, :], ident_f[:, :]).then_inc(consts, 1)
            pool.iota(iota_i, [[1, WCOL]], base=0, channel_multiplier=0).then_inc(iotas, 1)
            pool.iota(win_i, [[1, WIN_PAD]], base=0, channel_multiplier=0).then_inc(iotas, 1)
            pool.iota(after_i, [[1, CHUNKS]], base=1, channel_multiplier=0).then_inc(iotas, 1)
            pool.iota(part_a[:, 0:WIN_TILES], [[P * WIN, WIN_TILES]], base=0, channel_multiplier=WIN).then_inc(iotas, 1)
            pool.memset(sumT[:, :], 0.0).then_inc(zero_sums, 1)
            pool.sem_inc(res_ok, 1)
            with pool.Fori(0, GROUPS) as g:
                pool.wait_ge(y_ok, g + 1)
                pool.sem_inc(pool_turn, 1)
                pool.tensor_tensor(X[:, ds(g * GT, GT), :], X[:, ds(g * GT, GT), :], Y[:, :, :],
                                   ALU.add).then_inc(res_ok, 1)
                pool.wait_ge(hi_ok, g + 1)
                pool.sem_inc(pool_turn, 1)
                pool.tensor_tensor(v1p[:, 1, ds(g * GT, GT), :], v1[:, :, :], v1p[:, 0, ds(g * GT, GT), :],
                                   ALU.subtract).then_inc(v1_used, 1)

        @block.vector
        def _(dve):
            step = Steps(dve, scale_own)

            def then(ins):
                step.done(ins)
                step.wait()

            w1, b1 = W[:, :, D:], bias[:, D:]
            dve.wait_ge(w_in, 32)
            nc.vector.tensor_single_scalar(size[:, :, :].bitcast(i32), w1.bitcast(i32), 0x7fffffff, ALU.bitwise_and).then_inc(size_ok, 1)
            then(nc.vector.tensor_single_scalar(bound[:, :].bitcast(i32), b1.bitcast(i32), 0x7fffffff, ALU.bitwise_and))
            dve.wait_ge(size_sum, 1)
            then(nc.vector.scalar_tensor_tensor(bound[:, :], sps[:, 0:DN], float(D) ** 0.5, bound[:, :], ALU.mult, ALU.add))
            then(nc.vector.tensor_scalar(bound[:, :], bound[:, :], 1e-30, None, ALU.max))
            then(nc.vector.tensor_single_scalar(power[:, :], bound[:, :].bitcast(i32), 0x7f800000, ALU.bitwise_and))
            step.done(nc.vector.tensor_scalar(bound[:, :], power[:, :].bitcast(f32), 1.0 / LARGE, None, ALU.mult))
            then(nc.vector.tensor_scalar(recip[:, :], power[:, :], -1.0, float(ONE_OVER), ALU.mult, ALU.add))
            for k in range(2):
                step.done(nc.vector.scalar_tensor_tensor(W[:, k, D:], W[:, k, D:], LARGE, recip[:, :].bitcast(f32),
                                                         ALU.mult, ALU.mult))
            then(nc.vector.scalar_tensor_tensor(b1, b1, LARGE, recip[:, :].bitcast(f32), ALU.mult, ALU.mult))
            dve.sem_inc(w_ok, 1)
            dve.wait_ge(unscale_sum, 1)
            nc.vector.tensor_copy(unscale[:, :], sps[:, DN:DN + 1])

            own = Steps(dve, stat_own)

            def normalise(g, first=False):
                own.at(g * (GT + 1))
                dve.wait_ge(x_in, g * 16 + 16)
                dve.sem_inc(dve_turn, 1)
                for u in range(GT):
                    own.done(nc.vector.bn_stats(stats[:, u, :], flat2(X[:, ds(g * GT + u, 1), :])))
                own.wait()
                dve.sem_inc(dve_turn, 1)
                for u in range(GT):
                    nc.vector.bn_aggr(moments[:, u, :], stats[:, u, :]).then_inc(stats_ok, 1)
                dve.wait_ge(sqrt_ok, g + 1)
                own.done(nc.vector.reciprocal(rstd[:, :], rstd[:, :]))
                own.wait()
                if not first:
                    dve.wait_ge(tps_ok, g)
                    dve.sem_inc(dve_turn, 1)
                for u in range(GT):
                    last = nc.vector.tensor_scalar(XN[:, u, :], flat2(X[:, ds(g * GT + u, 1), :]),
                                                   moments[:, u, 0:1], rstd[:, u:u + 1], ALU.subtract, ALU.mult)
                last.then_inc(xn_ok, 1)

            def finish(g):
                dve.wait_ge(vps_ok, g + 1)
                dve.wait_ge(res_ok, g + 1)
                dve.sem_inc(dve_turn, 1)
                nc.vector.tensor_tensor(Y[:, :, :], vps[:, :, 0:D],
                                        bias[:, 0:D].unsqueeze(1).to_broadcast([P, GT, D]), ALU.add).then_inc(y_ok, 1)
                dve.wait_ge(v1_used, g + 1)
                nc.vector.tensor_tensor(v1[:, :, :], vps[:, :, D:D + DN],
                                        bias[:, D:].unsqueeze(1).to_broadcast([P, GT, DN]), ALU.add).then_inc(v1_ok, 1)
                dve.wait_ge(v1_ok, g + 1)
                dve.sem_inc(vps_free, 1)

            chain = Steps(dve, setup_own)

            def ready(ins):
                chain.done(ins)
                chain.wait()

            normalise(0, first=True)
            dve.wait_ge(iotas, 4)
            dve.wait_ge(edges_in, 48)
            nc.vector.tensor_copy(iota_row[:, :], iota_i[:, 0:P])
            nc.vector.tensor_copy(iota_col[:, :], iota_i)
            nc.vector.tensor_scalar(win_row[:, :], win_i, -float(P), None, ALU.mult)
            nc.vector.tensor_scalar(win_col[:, :], win_i, -float(WIN), None, ALU.mult)
            nc.vector.tensor_scalar(first_node[:, 0:WIN_TILES], part_a[:, 0:WIN_TILES], 1.0, None, ALU.mult)
            nc.vector.tensor_scalar(first_node[:, WIN_TILES:], part_a[:, 0:WIN_TILES], float(WIN), None, ALU.add)
            nc.vector.tensor_copy(after, after_i)
            ready(nc.vector.tensor_copy(dst_f, dst_by_chunk))
            by_chunk = dst_f.rearrange("p (c e) -> p c e", e=P)
            nc.vector.tensor_reduce(out=ends[:, 0:CHUNK_TILES], in_=by_chunk, op=ALU.min, axis=AX.X)
            nc.vector.tensor_reduce(out=ends[:, CHUNK_TILES:], in_=by_chunk, op=ALU.max, axis=AX.X).then_inc(ends_ok, 1)
            nc.vector.tensor_scalar(before, after, -1.0, float(CHUNKS + 1), ALU.mult, ALU.add)
            nc.vector.tensor_single_scalar(part_a, src_i, P - 1, ALU.bitwise_and)
            ready(nc.vector.tensor_single_scalar(part_b, dst_i, WIN.bit_length() - 1, ALU.arith_shift_right))
            ready(nc.vector.scalar_tensor_tensor(row_code[:, :], part_b, float(P), part_a, ALU.mult, ALU.add))
            ready(nc.vector.tensor_single_scalar(part_a, src_i, 7, ALU.arith_shift_right))
            ready(nc.vector.scalar_tensor_tensor(col_code[:, :], part_a, float(WIN), dst_i, ALU.mult, ALU.add))
            setup_steps = chain.n

            def window_ranges(q):
                chain.at(q * 4 + setup_steps)
                ready(nc.vector.scalar_tensor_tensor(found, max_row, first_node[:, ds(q, 1)], before, ALU.is_ge, ALU.mult))
                ready(nc.vector.tensor_reduce(out=spans[:, ds(q, 1)], in_=found, op=ALU.max, axis=AX.X))
                ready(nc.vector.scalar_tensor_tensor(found, min_row, first_node[:, ds(q + WIN_TILES, 1)],
                                                    after, ALU.is_lt, ALU.mult))
                ready(nc.vector.tensor_reduce(out=spans[:, ds(q + WIN_TILES, 1)], in_=found,
                                             op=ALU.max, axis=AX.X))

            with dve.Fori(0, GROUPS - 1 - WIN_TILES) as g:
                normalise(g + 1)
                finish(g)
            dve.wait_ge(rows_in, 32)
            with dve.Fori(GROUPS - 1 - WIN_TILES, GROUPS - 1) as g:
                normalise(g + 1)
                window_ranges(g - (GROUPS - 1 - WIN_TILES))
                finish(g)
            nc.vector.tensor_scalar(spans[:, 0:WIN_TILES], spans[:, 0:WIN_TILES], -1.0, float(CHUNKS),
                                    ALU.mult, ALU.add).then_inc(spans_ok, 1)
            finish(GROUPS - 1)

        @block.scalar
        def _(act):
            act.dma_start(W[:, :, :], w01.rearrange("(k p) n -> p k n", p=P)).then_inc(w_in, 16)
            act.dma_start(bias[:, :], b01.rearrange("(a n) -> a n", a=1).to_broadcast([P, D + DN])).then_inc(w_in, 16)
            act.wait_ge(consts, 3)

            def root(g):
                act.wait_ge(stats_ok, g * GT + GT)
                nc.scalar.activation(rstd[:, :], moments[:, :, 1], ACT.Sqrt, bias=eps[:, 0:1]).then_inc(sqrt_ok, 1)

            def turned_copy(g):
                act.wait_ge(tps_ok, g + 1)
                nc.scalar.copy(xT[:, :, :], tps[:, :, :]).then_inc(xT_ok, 1)

            def high_part(g):
                act.wait_ge(v1_ok, g + 1)
                act.sem_inc(act_turn, 1)
                nc.scalar.copy(v1p[:, 0, ds(g * GT, GT), :], v1[:, :, :]).then_inc(hi_ok, 1)

            act.sem_inc(v1_used, 1)
            root(0)
            with act.Fori(0, GROUPS - 1) as g:
                turned_copy(g)
                root(g + 1)
                high_part(g)
            turned_copy(GROUPS - 1)
            high_part(GROUPS - 1)

        @block.tensor
        def _(pe):
            pe.wait_ge(consts, 3)
            pe.wait_ge(size_ok, 1)
            for k in range(2):
                last = nc.tensor.matmul(sps[:, 0:DN], ones[:, :], size[:, k, :], start=(k == 0), stop=(k == 1))
            last.then_inc(size_sum, 1)
            pe.wait_ge(w_ok, 1)
            nc.tensor.matmul(sps[:, DN:DN + 1], bound[:, :], ident_f[:, 0:1], start=True, stop=True).then_inc(unscale_sum, 1)
            pe.sem_inc(vps_free, 1)
            with pe.Fori(0, GROUPS) as g:
                pe.wait_ge(xn_ok, g + 1)
                for u in range(GT):
                    for k in range(2):
                        last = nc.tensor.transpose(tps[:, k, u * P:(u + 1) * P],
                                                   XN[:, u, k * P:(k + 1) * P],
                                                   ident_f[:, :])
                last.then_inc(tps_ok, 1)
                pe.wait_ge(xT_ok, g + 1)
                pe.wait_ge(vps_free, g + 1)
                for u in range(GT):
                    for k in range(2):
                        last = nc.tensor.matmul(vps[:, u, 0:D + DN], xT[:, k, u * P:(u + 1) * P], W[:, k, :],
                                                start=(k == 0), stop=(k == 1))
                last.then_inc(vps_ok, 1)


def graph(nc, allocators, tables, v1p, unscale, sumT, ident_h,
          f32, f16, i32, ALU, ACT, AX, ds):
    with ExitStack() as ctx:
        sb, pb, sem = allocators(ctx)
        counts = [sb("counts_even", [P, SRC_PAD, BN], f16), sb("counts_odd", [P, SRC_PAD, BN], f16)]
        countsT = sb("countsT", [P, 2, CT * BLOCK], f16)
        src_hot = sb("src_hot", [P, 2, PAIR * UNIT + 1, P], f16)
        pair_hot = sb("pair_hot", [P, 2, PAIR * UNIT + 1, WCOL], f16)
        stage_s = sb("stage_s", [P, BLOCK], f32)
        stage_d = sb("stage_d", [P, BN], f32)
        tmp_a = sb("tmp_a", [1, WINDOWS], f32)
        tmp_b = sb("tmp_b", [1, WINDOWS], f32)
        firsts = sb("firsts", [1, WINDOWS], i32)
        extra = sb("extra", [1, WINDOWS], i32)
        v1_band = sb("v1_band", [P, 2, PARTS, CT * DN], f16)
        longest = sb("longest", [1, 2], f32)
        longest_i = sb("longest_i", [1, 2], i32)
        zeros = sb("zeros", [P, P], f16)
        row_code, col_code, iota_row, iota_col = tables["row_code"], tables["col_code"], tables["iota_row"], tables["iota_col"]
        win_row, win_col, lo_f, hi_f = tables["win_row"], tables["win_col"], tables["lo_f"], tables["hi_f"]
        win_ps = [pb("win_even", [P, 2, 512], f32), pb("win_odd", [P, 2, 512], f32)]
        turned = pb("turned", [P, 2 * 512], f32)
        dst_ps = pb("dst_ps", [P, 512], f32)
        src_ps = pb("src_ps", [P, 512], f32)

        own = sem("own")
        ranges_ok, longest_ok, ranges_used = sem("ranges_ok"), sem("longest_ok"), sem("ranges_used")
        hot_ok, hot_free, win_ok, win_free = sem("hot_ok"), sem("hot_free"), sem("win_ok"), sem("win_free")
        turned_ok, turned_free = sem("turned_ok"), sem("turned_free")
        src_ok, src_staged, src_added = sem("src_ok"), sem("src_staged"), sem("src_added")
        dst_ok, dst_staged, dst_added, zeroed = sem("dst_ok"), sem("dst_staged"), sem("dst_added"), sem("zeroed")
        band_ok, band_used = sem("band_ok"), sem("band_used")
        pe_turn, act_turn, dve_turn, pool_turn = (sem("g_pe_turn"), sem("g_act_turn"), sem("g_dve_turn"),
                                                  sem("g_pool_turn"))
        block = ctx.enter_context(nc.Block())

        def passes(eng):
            eng.wait_ge(longest_ok, 1)
            n = eng.value_load(longest_i[0:1, 0:1], min_val=1, max_val=CHUNKS)
            return eng.snap((n + (SUB - 1)) // SUB, min_val=1, max_val=CHUNKS // SUB + 1)

        def values(eng, table, w, n, low, high):
            return nc.values_load_multi_w_load_instructions(
                table[0:1, ds(w, n)], engines=[eng.engine], min_val=low, max_val=high,
                skip_runtime_bounds_check_because="DVE bounds them as it makes the table")[1]

        @block.gpsimd
        def _(pool):
            pool.memset(zeros[:, :], 0.0).then_inc(zeroed, 1)
            pool.sem_inc(src_added, 1)
            pool.sem_inc(dst_added, 1)
            n_pass = passes(pool)
            with pool.Fori(0, n_pass) as r:
                def fetch(g):
                    pool.wait_ge(band_used, r * BANDS + (g + 1))
                    pool.sem_inc(pool_turn, 1)
                    nc.gpsimd.tensor_copy(v1_band[:, ds(g % 2, 1), :, :].rearrange("p a b n -> p (a b) n"),
                                          v1p[:, :, ds(g * CT, CT), :].rearrange("p b t n -> p b (t n)")).then_inc(band_ok, 1)

                def add(g):
                    band = pool.snap(r * BANDS + g)
                    with pool.Fori(0, STEPS) as k:
                        pool.wait_ge(src_staged, band * BLOCKS + (k + 2))
                        pool.wait_ge(src_added, band * BLOCKS + (k + 1))
                        pool.wait_ge(dst_added, band + 1)
                        pool.sem_inc(pool_turn, 1)
                        v = sumT[:, ds(k * BLOCK, BLOCK)]
                        pool.tensor_tensor(v, v, stage_s[:, :], ALU.add).then_inc(src_added, 1)
                    pool.wait_ge(dst_staged, band + 2)
                    pool.wait_ge(src_added, band * BLOCKS + BLOCKS)
                    pool.sem_inc(pool_turn, 1)
                    v = sumT[:, ds(g * BN, BN)]
                    pool.tensor_tensor(v, v, stage_d[:, :], ALU.add).then_inc(dst_added, 1)
                    pool.wait_ge(dst_added, band + 2)
                    pool.sem_inc(pool_turn, 1)
                    pool.wait_ge(src_staged, band * BLOCKS + (BLOCKS + 1))
                    pool.sem_inc(pool_turn, 1)
                    v = sumT[:, (BLOCKS - 1) * BLOCK:BLOCKS * BLOCK]
                    pool.tensor_tensor(v, v, stage_s[:, :], ALU.add).then_inc(src_added, 1)

                pool.wait_ge(band_used, r * BANDS + 2)
                pool.sem_inc(pool_turn, 1)
                fetch(0)
                with pool.Fori(0, BANDS - 1) as g:
                    fetch(g + 1)
                    add(g)
                add(BANDS - 1)

        @block.vector
        def _(dve):
            step = Steps(dve, own)

            def then(ins):
                step.done(ins)
                step.wait()

            then(nc.vector.tensor_tensor(tmp_a[:, :], hi_f[:, :], lo_f[:, :], ALU.subtract))
            then(nc.vector.tensor_reduce(out=longest[:, 0:1], in_=tmp_a[:, :], op=ALU.max, axis=AX.X))
            then(nc.vector.tensor_scalar(longest[:, 1:2], longest[:, 0:1], 1.0, None, ALU.max))
            nc.vector.tensor_copy(longest_i[:, 0:1], longest[:, 1:2]).then_inc(longest_ok, 1)
            before_passes = step.n
            n_pass = passes(dve)
            made = dve.alloc_register("units_made")
            marks = [[dve.alloc_register(f"made_{a}_{b}") for b in ("first", "more")] for a in ("even", "odd")]
            for m in [made] + marks[0] + marks[1]:
                dve.reg_mov(m, 0)

            def hot(c, w, s, u):
                nc.vector.tensor_scalar(src_hot[:, s, u, :], iota_row[:, :], row_code[:, ds(c, 1)],
                                        win_row[:, ds(w, 1)], ALU.subtract, ALU.is_equal)
                return nc.vector.tensor_scalar(pair_hot[:, s, u, :], iota_col[:, :], col_code[:, ds(c, 1)],
                                               win_col[:, ds(w, 1)], ALU.subtract, ALU.is_equal)

            def unit(hots, mark):
                dve.wait_ge(hot_free, dve.snap(mark) + 1)
                dve.sem_inc(dve_turn, 1)
                for h in hots:
                    last = hot(*h)
                last.then_inc(hot_ok, 1)
                dve.reg_add(made, made, 1)
                dve.reg_mov(mark, made)

            with dve.Fori(0, n_pass) as r:
                step.at(r * RANGE_STEPS + before_passes)
                dve.wait_ge(ranges_used, r + 1)
                then(nc.vector.tensor_tensor(tmp_a[:, :], lo_f[:, :], hi_f[:, :], ALU.is_lt))
                then(nc.vector.tensor_scalar(tmp_b[:, :], lo_f[:, :], float(-CHUNKS), None, ALU.add))
                then(nc.vector.tensor_tensor(tmp_b[:, :], tmp_b[:, :], tmp_a[:, :], ALU.mult))
                then(nc.vector.tensor_scalar(firsts[:, :], tmp_b[:, :], float(CHUNKS), None, ALU.add))
                then(nc.vector.tensor_tensor(tmp_b[:, :], hi_f[:, :], lo_f[:, :], ALU.subtract))
                then(nc.vector.tensor_scalar(lo_f[:, :], lo_f[:, :], float(SUB), None, ALU.add))
                then(nc.vector.tensor_scalar(tmp_b[:, :], tmp_b[:, :], float(UNIT), float(SUB), ALU.max, ALU.min))
                then(nc.vector.tensor_scalar(tmp_b[:, :], tmp_b[:, :], float(-UNIT), None, ALU.add))
                then(nc.vector.tensor_copy(extra[:, :], tmp_b[:, :]))
                assert step.n == RANGE_STEPS
                dve.sem_inc(ranges_ok, 1)
                with dve.Fori(0, WINDOWS // LOAD) as part:
                    lo = values(dve, firsts, part * LOAD, LOAD, 0, CHUNKS)
                    n = values(dve, extra, part * LOAD, LOAD, 0, SUB - UNIT)
                    for k in range(0, LOAD, PAIR):
                        s = k // PAIR % 2
                        w = [dve.snap(part * LOAD + (k + b), min_val=0, max_val=WINDOWS - 1) for b in range(PAIR)]
                        unit([(lo[k + b] + u, w[b], s, b * UNIT + u) for b in range(PAIR) for u in range(UNIT)],
                             marks[s][0])
                        with dve.If(n[k] + n[k + 1] > 0):
                            for b in range(PAIR):
                                with dve.If(n[k + b] > 0):
                                    with dve.Fori(0, n[k + b]) as m:
                                        c = dve.snap(lo[k + b] + m + UNIT, min_val=0, max_val=CHUNKS + SUB)
                                        unit([(c, w[b], s, PAIR * UNIT)], marks[s][1])

        @block.scalar
        def _(act):
            act.sem_inc(win_free, 2)
            act.sem_inc(turned_free, 1)
            act.sem_inc(src_staged, 1)
            act.sem_inc(dst_staged, 1)
            n_pass = passes(act)

            def window(built, k, s, buf):
                act.wait_ge(win_ok, built * STEPS + (k + 1))
                act.sem_inc(act_turn, 1)
                nc.scalar.copy(counts[buf][:, :, ds(k * (PAIR * WIN), PAIR * WIN)].rearrange("p h (b w) -> p b h w", b=PAIR),
                               win_ps[s][:, :, 0:WCOL].rearrange("p b (h w) -> p b h w", w=WIN)).then_inc(win_free, 1)

            def turned_copy(band, k, s):
                act.wait_ge(turned_ok, band * BLOCKS + (k + 1))
                nc.scalar.copy(countsT[:, s, :], turned[:, 0:CT * BLOCK]).then_inc(turned_free, 1)

            def sources(band, k):
                act.wait_ge(src_ok, band * BLOCKS + (k + 1))
                act.wait_ge(src_added, band * BLOCKS + (k + 1))
                nc.scalar.activation(stage_s[:, :], src_ps[:, 0:BLOCK], ACT.Copy, scale=unscale[:, 0:1]).then_inc(src_staged, 1)

            def multiply_step(band, k, s):
                turned_copy(band, k + 1, 1 - s)
                sources(band, k)

            def end_of_band(band):
                act.wait_ge(dst_ok, band + 1)
                act.wait_ge(dst_added, band + 1)
                nc.scalar.activation(stage_d[:, :], dst_ps[:, 0:BN], ACT.Copy, scale=unscale[:, 0:1]).then_inc(dst_staged, 1)
                sources(band, BLOCKS - 1)

            with act.Fori(0, n_pass) as r:
                with act.Fori(0, STEPS // 2) as q:
                    for s in range(2):
                        window(r * BANDS, q * 2 + s, s, 0)
                with act.Fori(0, BANDS // 2) as i:
                    for odd in range(2):
                        band = act.snap(r * BANDS + i * 2 + odd)
                        turned_copy(band, 0, 0)
                        with act.Fori(0, STEPS // 2) as q:
                            for s in range(2):
                                window(band + 1, q * 2 + s, s, 1 - odd)
                                multiply_step(band, q * 2 + s, s)
                        end_of_band(band)
                band = act.snap(r * BANDS + (BANDS - 1))
                turned_copy(band, 0, 0)
                with act.Fori(0, STEPS // 2) as q:
                    for s in range(2):
                        multiply_step(band, q * 2 + s, s)
                end_of_band(band)

        @block.tensor
        def _(pe):
            pe.wait_ge(zeroed, 1)
            pe.sem_inc(hot_free, 1)
            pe.sem_inc(ranges_used, 1)
            pe.sem_inc(band_used, 2)
            n_pass = passes(pe)
            seen = pe.alloc_register("units_seen")
            pe.reg_mov(seen, 0)

            def count_unit(ps, s, hots):
                pe.reg_add(seen, seen, 1)
                pe.wait_ge(hot_ok, pe.snap(seen))
                for b, u in hots:
                    last = nc.tensor.matmul(ps[:, b, 0:WCOL], src_hot[:, s, u, :], pair_hot[:, s, u, :],
                                            start=False, stop=False)
                last.then_inc(hot_free, 1)

            def windows(built, k, n):
                ps = win_ps[k % 2]
                pe.wait_ge(win_free, built * STEPS + (k + 1))
                for b in range(PAIR):
                    nc.tensor.matmul(ps[:, b, WCOL:WCOL + 1], zeros[:, :], zeros[:, 0:1], start=True, stop=False)
                count_unit(ps, k % 2, [(b, b * UNIT + u) for b in range(PAIR) for u in range(UNIT)])
                with pe.If(n[0] + n[1] > 0):
                    for b in range(PAIR):
                        with pe.If(n[b] > 0):
                            with pe.Fori(0, n[b]) as _:
                                count_unit(ps, k % 2, [(b, PAIR * UNIT)])
                for b in range(PAIR):
                    last = nc.tensor.matmul(ps[:, b, WCOL:WCOL + 1], zeros[:, :], zeros[:, 0:1], start=False, stop=True)
                last.then_inc(win_ok, 1)

            def turn(k, buf):
                for t in range(CT):
                    for u in range(BT):
                        last = nc.tensor.matmul(turned[:, (t * BT + u) * P:(t * BT + u + 1) * P],
                                                counts[buf][:, k * BT + u, t * P:(t + 1) * P],
                                                ident_h[:, :], start=True, stop=True)
                last.then_inc(turned_ok, 1)

            def to_destinations(k, buf, final=False):
                for u in range(BT):
                    for part in range(PARTS):
                        last = nc.tensor.matmul(dst_ps[:, 0:BN], v1p[:, part, k * BT + u, :], counts[buf][:, k * BT + u, :],
                                                start=(k == 0 and u == 0 and part == 0),
                                                stop=(final and u == BT - 1 and part == PARTS - 1))
                return last

            def to_sources(band, k, buf):
                pe.wait_ge(src_staged, band * BLOCKS + (k + 1))
                for t in range(CT):
                    for part in range(PARTS):
                        last = nc.tensor.matmul(src_ps[:, 0:BLOCK], v1_band[:, buf, part, t * DN:(t + 1) * DN],
                                                countsT[:, k % 2, t * BLOCK:(t + 1) * BLOCK],
                                                start=(t == 0 and part == 0), stop=(t == CT - 1 and part == PARTS - 1))
                return last.then_inc(src_ok, 1)

            def stage(band, buf, built, g_built):
                pe.wait_ge(band_ok, band + 1)
                pe.wait_ge(win_free, band * STEPS + (STEPS + 2))
                pe.wait_ge(dst_staged, band + 1)
                pe.wait_ge(turned_free, band * BLOCKS + 1)
                turn(0, buf)
                n = None
                for k in range(STEPS):
                    if built is not None:
                        at = k * PAIR % LOAD
                        if at == 0:
                            n = values(pe, extra, g_built * WPB + k * PAIR, LOAD, 0, SUB - UNIT)
                        windows(built, k, n[at:at + PAIR])
                    to_destinations(k, buf)
                    pe.wait_ge(turned_free, band * BLOCKS + (k + 2))
                    turn(k + 1, buf)
                    to_sources(band, k, buf)
                to_destinations(BLOCKS - 1, buf, True).then_inc(dst_ok, 1)
                pe.wait_ge(turned_free, band * BLOCKS + (BLOCKS + 1))
                to_sources(band, BLOCKS - 1, buf)
                pe.sem_inc(band_used, 1)

            with pe.Fori(0, n_pass) as r:
                pe.wait_ge(ranges_ok, r + 1)
                pe.sem_inc(pe_turn, 1)
                for h in range(WPB // LOAD):
                    n = values(pe, extra, h * LOAD, LOAD, 0, SUB - UNIT)
                    for k in range(LOAD // PAIR):
                        windows(pe.snap(r * BANDS), h * (LOAD // PAIR) + k, n[k * PAIR:(k + 1) * PAIR])
                with pe.Fori(0, BANDS // 2) as i:
                    for odd in range(2):
                        band = pe.snap(r * BANDS + i * 2 + odd)
                        stage(band, odd, pe.snap(band + 1), pe.snap(i * 2 + (odd + 1)))
                stage(pe.snap(r * BANDS + (BANDS - 1)), 0, None, None)
                pe.sem_inc(ranges_used, 1)


def ffn(nc, allocators, residual, sumT, ident_f, W1, b1, Wg, bg, Wd, bd, out,
        f32, f16, i32, ALU, ACT, AX, ds):
    with ExitStack() as ctx:
        sb, _, _ = allocators(ctx)
        rows = nc.dram_tensor("rows", [TILES * P, 2 * D], f32, kind="Internal").ap()
        w1 = sb("w1", [P, K1, HID], f32)
        b1c = sb("b1c", [P, KH], f32)
        wd = sb("wd", [P, KH, EXPERTS * D], f32)
        bdr = sb("bdr", [P, EXPERTS * D], f32)
        expert = sb("expert", [P, SLOT_TILES], i32)
        who = dict(read=sb("who_read", [P, SLOT_TILES], i32), write=sb("who_write", [P, SLOT_TILES], i32),
                   weight=sb("who_weight", [P, SLOT_TILES], f32))
        route(nc, allocators, residual, sumT, ident_f, W1, b1, Wg, bg, Wd, bd, rows, who, w1, b1c, wd, bdr, expert,
              f32, i32, ALU, ACT, AX, ds)
        experts(nc, allocators, ident_f, rows, who, w1, b1c, wd, bdr, expert, out,
                f32, i32, ALU, ACT, AX, ds)


def spread(ap, shape):
    return ap.unsqueeze(2).to_broadcast(shape)


def route(nc, allocators, residual, sumT, ident_f, W1, b1, Wg, bg, Wd, bd, rows, who, w1, b1c, wd, bdr, expert,
          f32, i32, ALU, ACT, AX, ds):
    with ExitStack() as ctx:
        sb, pb, sem = allocators(ctx)
        X = sb("rX", [P, TILES, D], f32)
        XN = sb("rXN", [P, GT, D], f32)
        nbT = sb("nbT", [P, GN], f32)
        wg = sb("wg", [P, KH, EXPERTS], f32)
        bgr = sb("bgr", [P, EXPERTS], f32)
        eps = sb("r_eps", [P, 1], f32)
        stats = sb("r_stats", [P, GT, 6], f32)
        mv = sb("r_mv", [P, GT, 2], f32)
        rstd = sb("r_rstd", [P, GT], f32)
        xT = sb("r_xT", [P, K1, GN], f32)
        H = sb("r_H", [P, KH, GN], f32)
        logits = sb("logits", [P, TILES, EXPERTS], f32)
        hflat = H[:, :, :].rearrange("p a b -> p (a b)")
        taken = [0]

        def take(*dims):
            n = dims[0] * (dims[1] if len(dims) > 1 else 1)
            taken[0] += n
            v = hflat[:, taken[0] - n:taken[0]]
            return v.rearrange("p (a b) -> p a b", b=dims[1]) if len(dims) > 1 else v

        TE = (TILES, EXPERTS)
        expo, prob, cand, sel, place = take(*TE), take(*TE), take(*TE), take(*TE), take(*TE)
        scan = [take(*TE), take(*TE)]
        per_tile = take(SLOT_TILES, EXPERTS)
        top, weight, tok, valid, pos = (take(TILES) for _ in range(5))
        tiles_of, ends, ends_b, base = (take(EXPERTS) for _ in range(4))
        tiles_i = take(EXPERTS).bitcast(i32)
        expert_f = take(SLOT_TILES)
        rank = sb("rank", [P, EXPERTS], f32)
        slot_no = sb("slot_no", [P, SLOT_TILES], f32)
        earlier = sb("earlier", [P, P], f32)
        ones = sb("ones", [P, P], f32)
        ints = sb("ints", [P, TILES + SLOT_TILES + EXPERTS], i32)
        lanes = sb("lanes", [P, P], i32)
        lane_no = sb("lane_no", [P, P], f32)
        pos_i = sb("pos_i", [P, TILES], i32)
        tile_i = sb("tile_i", [P, TILES], i32)
        xflat = X[:, :, :].rearrange("p a b -> p (a b)")
        in_lane = xflat[:, 0:TILES * P].rearrange("p (t l) -> p t l", l=P)
        in_tile = xflat[:, TILES * P:TILES * (P + 2 * SLOT_TILES)].rearrange("p (t v n) -> p t v n", v=2, n=SLOT_TILES)
        nb = pb("nb", [P, GN], f32)
        up = pb("r_up", [P, 2, 512], f32)
        tps = pb("r_tps", [P, K1, GN], f32)
        gate = pb("gate", [P, GT, EXPERTS], f32)
        before_ps = pb("before_ps", [P, 512], f32)
        total_ps = pb("total_ps", [P, 512], f32)

        x_in, w_in, wd_in, consts, own = sem("r_x_in"), sem("r_w_in"), sem("wd_in"), sem("r_consts"), sem("r_own")
        nb_in, nb_ok, nb_used = sem("nb_in"), sem("nb_ok"), sem("nb_used")
        var_ok, std_ok, xn_ok, rows_out = sem("var_ok"), sem("std_ok"), sem("r_xn_ok"), sem("rows_out")
        tps_ok, xT_ok, up_ok, h_ok, gate_ok, gate_used = (sem("r_tps_ok"), sem("r_xT_ok"), sem("up_ok"), sem("h_ok"),
                                                          sem("gate_ok"), sem("gate_used"))
        shift_ok, exp_ok, sel_ok, ranks_ok = sem("shift_ok"), sem("exp_ok"), sem("sel_ok"), sem("ranks_ok")
        hot_ok, sorted_ok = sem("r_hot_ok"), sem("sorted_ok")
        pe_turn, act_turn, dve_turn, pool_turn, pool_own = (sem("r_pe_turn"), sem("r_act_turn"), sem("r_dve_turn"),
                                                            sem("r_pool_turn"), sem("r_pool_own"))
        block = ctx.enter_context(nc.Block())
        res_t = residual.rearrange("(t p) d -> p t d", p=P)
        rows_t = rows.rearrange("(t p) d -> p t d", p=P)

        def row(a, n):
            return a.rearrange("(a n) -> a n", a=1).to_broadcast([P, n])

        @block.sync
        def _(sp):
            def load(g):
                sp.wait_ge(x_in, g * 16)
                sp.dma_start(X[:, ds(g * GT, GT), :], res_t[:, ds(g * GT, GT), :]).then_inc(x_in, 16)

            def store(g):
                sp.wait_ge(xn_ok, g + 1)
                sp.dma_start(rows_t[:, ds(g * GT, GT), 0:D], X[:, ds(g * GT, GT), :]).then_inc(rows_out, 16)
                sp.dma_start(rows_t[:, ds(g * GT, GT), D:2 * D], XN[:, :, :]).then_inc(rows_out, 16)

            sp.dma_start(X[:, 0:GT, :], res_t[:, 0:GT, :]).then_inc(x_in, 16)
            for g in range(1, AHEAD):
                load(g)
            with sp.Fori(0, GROUPS - AHEAD) as g:
                store(g)
                load(g + AHEAD)
            with sp.Fori(GROUPS - AHEAD, GROUPS) as g:
                store(g)
            sp.wait_ge(rows_out, GROUPS * 32)

        @block.gpsimd
        def _(pool):
            pool.memset(eps[:, :], EPS).then_inc(consts, 1)
            pool.memset(ones[:, :], 1.0).then_inc(pool_own, 1)
            pool.wait_ge(pool_own, 1)
            pool.affine_select(out=earlier[:, :], in_=ones[:, :], compare_op=ALU.is_gt, fill=0.0,
                               base=0, pattern=[[1, P]], channel_multiplier=-1).then_inc(consts, 1)
            pool.iota(ints[:, 0:TILES], [[P, TILES]], base=0, channel_multiplier=1).then_inc(pool_own, 1)
            pool.iota(ints[:, TILES:TILES + SLOT_TILES], [[1, SLOT_TILES]], base=0, channel_multiplier=0).then_inc(pool_own, 1)
            pool.iota(ints[:, TILES + SLOT_TILES:], [[-1, EXPERTS]], base=EXPERTS, channel_multiplier=0).then_inc(pool_own, 1)
            pool.iota(lanes[:, :], [[1, P]], base=0, channel_multiplier=0).then_inc(pool_own, 1)
            pool.wait_ge(pool_own, 5)
            pool.tensor_copy(slot_no[:, :], ints[:, TILES:TILES + SLOT_TILES]).then_inc(consts, 1)
            pool.tensor_copy(rank[:, :], ints[:, TILES + SLOT_TILES:]).then_inc(consts, 1)
            pool.tensor_copy(lane_no[:, :], lanes[:, :]).then_inc(consts, 1)
            pool.tensor_copy(nbT[:, :], sumT[:, 0:GN]).then_inc(nb_in, 1)
            with pool.Fori(1, GROUPS) as g:
                pool.wait_ge(nb_ok, g)
                pool.sem_inc(pool_turn, 1)
                pool.tensor_copy(nbT[:, :], sumT[:, ds(g * GN, GN)]).then_inc(nb_in, 1)

        @block.vector
        def _(dve):
            step = Steps(dve, own)

            def then(ins):
                step.done(ins)
                step.wait()

            def variance(g):
                step.at(g * (GT + 2))
                dve.wait_ge(x_in, g * 16 + 16)
                dve.wait_ge(nb_ok, g + 1)
                dve.sem_inc(dve_turn, 1)
                x = X[:, ds(g * GT, GT), 0:DN]
                then(nc.vector.tensor_tensor(x, x, nb[:, :].rearrange("p (t n) -> p t n", n=DN), ALU.add))
                dve.sem_inc(nb_used, 1)
                for t in range(GT):
                    step.done(nc.vector.bn_stats(stats[:, t, :], flat2(X[:, ds(g * GT + t, 1), :])))
                step.wait()
                dve.sem_inc(dve_turn, 1)
                for t in range(GT):
                    nc.vector.bn_aggr(mv[:, t, :], stats[:, t, :]).then_inc(var_ok, 1)

            def normalise(g, first=False):
                dve.wait_ge(std_ok, g + 1)
                step.at(g * (GT + 2) + (GT + 1))
                then(nc.vector.reciprocal(rstd[:, :], rstd[:, :]))
                if not first:
                    dve.wait_ge(tps_ok, g)
                    dve.wait_ge(rows_out, g * 32)
                    dve.sem_inc(dve_turn, 1)
                for u in range(GT):
                    last = nc.vector.tensor_scalar(XN[:, u, :], flat2(X[:, ds(g * GT + u, 1), :]),
                                                   mv[:, u, 0:1], rstd[:, u:u + 1], ALU.subtract, ALU.mult)
                last.then_inc(xn_ok, 1)

            def add_bias(g):
                dve.wait_ge(gate_ok, g + 1)
                dve.sem_inc(dve_turn, 1)
                nc.vector.tensor_tensor(logits[:, ds(g * GT, GT), :], gate[:, :, :],
                                        bgr[:, :].unsqueeze(1).to_broadcast([P, GT, EXPERTS]), ALU.add).then_inc(gate_used, 1)

            def copy_turned(g):
                dve.wait_ge(tps_ok, g + 1)
                nc.vector.tensor_copy(xT[:, :, :], tps[:, :, :]).then_inc(xT_ok, 1)

            variance(0)
            normalise(0, first=True)
            copy_turned(0)
            variance(1)
            normalise(1)
            dve.wait_ge(w_in, 16 * 4)
            with dve.Fori(0, GROUPS - 2) as g:
                variance(g + 2)
                copy_turned(g + 1)
                normalise(g + 2)
                add_bias(g)
            copy_turned(GROUPS - 1)
            add_bias(GROUPS - 2)
            add_bias(GROUPS - 1)
            step.at(GROUPS * (GT + 2))
            dve.wait_ge(gate_used, GROUPS + 1)
            shape = [P, TILES, EXPERTS]
            then(nc.vector.tensor_reduce(out=top, in_=logits[:, :, :], op=ALU.max, axis=AX.X))
            nc.vector.tensor_tensor(cand, logits[:, :, :], spread(top, shape), ALU.subtract).then_inc(shift_ok, 1)
            dve.wait_ge(exp_ok, 1)
            then(nc.vector.tensor_reduce(out=top, in_=expo, op=ALU.add, axis=AX.X))
            then(nc.vector.reciprocal(top, top))
            then(nc.vector.tensor_tensor(prob, expo, spread(top, shape), ALU.mult))
            dve.wait_ge(consts, 5)
            then(nc.vector.tensor_reduce(out=weight, in_=prob, op=ALU.max, axis=AX.X))
            then(nc.vector.tensor_tensor(cand, prob, spread(weight, shape), ALU.is_equal))
            then(nc.vector.tensor_tensor(cand, cand, rank[:, :].unsqueeze(1).to_broadcast(shape), ALU.mult))
            then(nc.vector.tensor_reduce(out=top, in_=cand, op=ALU.max, axis=AX.X))
            step.done(nc.vector.tensor_tensor(sel, cand, spread(top, shape), ALU.is_equal))
            then(nc.vector.tensor_scalar(valid, ints[:, 0:TILES], float(NODES), None, ALU.is_lt))
            then(nc.vector.tensor_tensor(sel, sel, spread(valid, shape), ALU.mult))
            dve.sem_inc(sel_ok, 1)
            dve.wait_ge(ranks_ok, 1)
            total = total_ps[:, 0:TILES * EXPERTS].rearrange("p (t e) -> p t e", e=EXPERTS)
            before = before_ps[:, 0:TILES * EXPERTS].rearrange("p (t e) -> p t e", e=EXPERTS)
            then(nc.vector.tensor_copy(scan[0], total))
            a, b, far = 0, 1, 1
            while far < TILES:
                step.done(nc.vector.tensor_copy(scan[b][:, 0:far, :], scan[a][:, 0:far, :]))
                then(nc.vector.tensor_tensor(scan[b][:, far:, :], scan[a][:, far:, :], scan[a][:, 0:TILES - far, :], ALU.add))
                a, b, far = b, a, 2 * far
            then(nc.vector.tensor_scalar(tiles_of, scan[a][:, TILES - 1, :], float(P - 1), None, ALU.add))
            then(nc.vector.tensor_copy(tiles_i, tiles_of))
            then(nc.vector.tensor_single_scalar(tiles_i, tiles_i, 7, ALU.arith_shift_right))
            then(nc.vector.tensor_copy(tiles_of, tiles_i))
            then(nc.vector.tensor_copy(ends, tiles_of))
            e0, e1, far = ends, ends_b, 1
            while far < EXPERTS:
                step.done(nc.vector.tensor_copy(e1[:, 0:far], e0[:, 0:far]))
                then(nc.vector.tensor_tensor(e1[:, far:], e0[:, far:], e0[:, 0:EXPERTS - far], ALU.add))
                e0, e1, far = e1, e0, 2 * far
            then(nc.vector.tensor_tensor(base, e0, tiles_of, ALU.subtract))
            then(nc.vector.tensor_scalar(base, base, float(P), None, ALU.mult))
            then(nc.vector.tensor_tensor(place, scan[a], total, ALU.subtract))
            then(nc.vector.tensor_tensor(place, place, before, ALU.add))
            then(nc.vector.tensor_tensor(place, place, base.unsqueeze(1).to_broadcast(shape), ALU.add))
            then(nc.vector.tensor_tensor(place, place, sel, ALU.mult))
            step.done(nc.vector.tensor_reduce(out=pos, in_=place, op=ALU.add, axis=AX.X))
            then(nc.vector.tensor_scalar(valid, valid, -float(NOWHERE), float(NOWHERE), ALU.mult, ALU.add))
            then(nc.vector.tensor_tensor(pos, pos, valid, ALU.add))
            then(nc.vector.tensor_copy(pos_i[:, :], pos))
            step.done(nc.vector.tensor_single_scalar(tile_i[:, :], pos_i[:, :], 7, ALU.arith_shift_right))
            then(nc.vector.tensor_single_scalar(pos_i[:, :], pos_i[:, :], P - 1, ALU.bitwise_and))
            step.done(nc.vector.tensor_copy(pos, pos_i[:, :]))
            step.done(nc.vector.tensor_copy(valid, tile_i[:, :]))
            then(nc.vector.tensor_scalar(tok, ints[:, 0:TILES], 1.0, None, ALU.add))
            dve.wait_ge(rows_out, GROUPS * 32)
            for c in range(GT):
                at = slice(c * GROUPS, (c + 1) * GROUPS)
                lane_shape, tile_shape = [P, GROUPS, P], [P, GROUPS, SLOT_TILES]
                step.done(nc.vector.tensor_tensor(in_lane[:, at, :], spread(pos[:, at], lane_shape),
                                                  lane_no[:, :].unsqueeze(1).to_broadcast(lane_shape), ALU.is_equal))
                then(nc.vector.tensor_tensor(in_tile[:, at, 0, :], spread(valid[:, at], tile_shape),
                                             slot_no[:, :].unsqueeze(1).to_broadcast(tile_shape), ALU.is_equal))
                then(nc.vector.tensor_tensor(in_tile[:, at, 1, :], in_tile[:, at, 0, :],
                                             spread(weight[:, at], tile_shape), ALU.mult))
                nc.vector.tensor_tensor(in_tile[:, at, 0, :], in_tile[:, at, 0, :],
                                        spread(tok[:, at], tile_shape), ALU.mult).then_inc(hot_ok, 1)
            eshape = [P, SLOT_TILES, EXPERTS]
            then(nc.vector.tensor_tensor(per_tile, spread(slot_no[:, :], eshape), e0.unsqueeze(1).to_broadcast(eshape), ALU.is_ge))
            then(nc.vector.tensor_reduce(out=expert_f, in_=per_tile, op=ALU.add, axis=AX.X))
            then(nc.vector.tensor_scalar(expert_f, expert_f, float(EXPERTS - 1), None, ALU.min))
            then(nc.vector.tensor_copy(expert[:, :], expert_f))
            dve.wait_ge(sorted_ok, 1)
            found = before_ps[:, 0:SLOT_TILES]
            step.done(nc.vector.tensor_copy(who["weight"][:, :], before_ps[:, SLOT_TILES:2 * SLOT_TILES]))
            then(nc.vector.tensor_scalar(expert_f, found, 1.0, None, ALU.is_lt))
            step.done(nc.vector.scalar_tensor_tensor(slot_no[:, :], expert_f, float(NODES + 1), found, ALU.mult, ALU.add))
            then(nc.vector.scalar_tensor_tensor(expert_f, expert_f, float(NOWHERE), found, ALU.mult, ALU.add))
            step.done(nc.vector.tensor_scalar(who["read"][:, :], slot_no[:, :], -1.0, None, ALU.add))
            then(nc.vector.tensor_scalar(who["write"][:, :], expert_f, -1.0, None, ALU.add))

        @block.scalar
        def _(act):
            act.dma_start(w1[:, :, :], W1.rearrange("(k p) n -> p k n", p=P)).then_inc(w_in, 16)
            with nc.allow_non_contiguous_dma(reason="a word per hidden feature, once"):
                act.dma_start(b1c[:, :], b1.rearrange("(k p) -> p k", p=P)).then_inc(w_in, 16)
            act.dma_start(wg[:, :, :], Wg.rearrange("(k p) n -> p k n", p=P)).then_inc(w_in, 16)
            act.dma_start(bgr[:, :], row(bg, EXPERTS)).then_inc(w_in, 16)
            act.dma_start(bdr[:, :], row(bd.rearrange("e d -> (e d)"), EXPERTS * D)).then_inc(wd_in, 16)
            for e in range(EXPERTS):
                act.dma_start(wd[:, :, e * D:(e + 1) * D], Wd[e, :, :].rearrange("(k p) n -> p k n", p=P)).then_inc(wd_in, 16)
            act.wait_ge(consts, 1)

            def root(g):
                act.wait_ge(var_ok, g * GT + GT)
                nc.scalar.activation(rstd[:, :], mv[:, :, 1], ACT.Sqrt, bias=eps[:, 0:1]).then_inc(std_ok, 1)

            def gelus(g):
                for j in range(KH):
                    act.wait_ge(up_ok, g * KH + (j + 1))
                    nc.scalar.activation(H[:, j, :], up[:, j % 2, :], ACT.Gelu, bias=b1c[:, j:j + 1]).then_inc(h_ok, 1)

            root(0)
            root(1)
            act.wait_ge(w_in, 16 * 4)
            with act.Fori(0, GROUPS - 2) as g:
                gelus(g)
                root(g + 2)
            gelus(GROUPS - 2)
            gelus(GROUPS - 1)
            act.wait_ge(gate_ok, GROUPS)
            act.wait_ge(shift_ok, 1)
            nc.scalar.activation(expo, cand, ACT.Exp).then_inc(exp_ok, 1)
            act.wait_ge(wd_in, 16 * (EXPERTS + 1))

        @block.tensor
        def _(pe):
            pe.sem_inc(nb_used, 1)

            def turn_sums(g):
                pe.wait_ge(nb_in, g + 1)
                pe.wait_ge(nb_used, g + 1)
                for t in range(GT):
                    last = nc.tensor.transpose(nb[:, t * P:(t + 1) * P], nbT[:, t * P:(t + 1) * P], ident_f[:, :])
                last.then_inc(nb_ok, 1)

            turn_sums(0)
            pe.wait_ge(w_in, 16 * 4)
            pe.sem_inc(gate_used, 1)

            def turn(g):
                pe.wait_ge(xn_ok, g + 1)
                for t in range(GT):
                    for k in range(K1):
                        last = nc.tensor.transpose(tps[:, k, t * P:(t + 1) * P], XN[:, t, k * P:(k + 1) * P], ident_f[:, :])
                last.then_inc(tps_ok, 1)

            def hidden(g):
                pe.wait_ge(xT_ok, g + 1)
                for j in range(KH):
                    pe.wait_ge(h_ok, g * KH + (j - 1 + 2))
                    for k in range(K1):
                        last = nc.tensor.matmul(up[:, j % 2, :], w1[:, k, j * P:(j + 1) * P], xT[:, k, :],
                                                start=(k == 0), stop=(k == K1 - 1))
                    last.then_inc(up_ok, 1)

            def logit(g):
                pe.wait_ge(h_ok, g * KH + (KH + 2))
                pe.wait_ge(gate_used, g + 1)
                for t in range(GT):
                    for j in range(KH):
                        last = nc.tensor.matmul(gate[:, t, :], H[:, j, t * P:(t + 1) * P], wg[:, j, :],
                                                start=(j == 0), stop=(j == KH - 1))
                last.then_inc(gate_ok, 1)

            pe.sem_inc(h_ok, 2)
            turn(0)
            turn_sums(1)
            with pe.Fori(0, GROUPS - 2) as g:
                turn_sums(g + 2)
                hidden(g)
                turn(g + 1)
                logit(g)
            hidden(GROUPS - 2)
            turn(GROUPS - 1)
            logit(GROUPS - 2)
            hidden(GROUPS - 1)
            logit(GROUPS - 1)
            pe.wait_ge(sel_ok, 1)
            pe.wait_ge(consts, 5)
            flat_sel = sel.rearrange("p t e -> p (t e)")
            nc.tensor.matmul(before_ps[:, 0:TILES * EXPERTS], earlier[:, :], flat_sel, start=True, stop=True)
            nc.tensor.matmul(total_ps[:, 0:TILES * EXPERTS], ones[:, :], flat_sel, start=True, stop=True).then_inc(ranks_ok, 1)
            for t in range(TILES):
                if t % GROUPS == 0:
                    pe.wait_ge(hot_ok, t // GROUPS + 1)
                last = nc.tensor.matmul(before_ps[:, 0:2 * SLOT_TILES], in_lane[:, t, :],
                                        in_tile[:, t, :, :].rearrange("p v n -> p (v n)"),
                                        start=(t == 0), stop=(t == TILES - 1))
            last.then_inc(sorted_ok, 1)


def experts(nc, allocators, ident_f, rows, who, w1, b1c, wd, bdr, expert, out,
            f32, i32, ALU, ACT, AX, ds):
    with ExitStack() as ctx:
        sb, pb, sem = allocators(ctx)
        R = sb("R", [P, 2, GT, 2 * D], f32)
        from_row = sb("from_row", [P, 2, GT], i32)
        to_row = sb("to_row", [P, 2, GT], i32)
        xT = sb("e_xT", [P, K1, GN], f32)
        H = sb("e_H", [P, KH, GN], f32)
        Y = sb("e_Y", [P, 2, GT, D], f32)
        up = pb("e_up", [P, 2, 512], f32)
        tps = pb("e_tps", [P, K1, GN], f32)
        down = pb("down", [P, 2, 512], f32)

        idx_ok = sem("idx_ok")
        row_in = [sem("row_in0"), sem("row_in1")]
        row_out = [sem("row_out0"), sem("row_out1")]
        tps_ok, xT_ok, up_ok, h_ok = sem("e_tps_ok"), sem("e_xT_ok"), sem("e_up_ok"), sem("e_h_ok")
        down_ok, down_used, y_ok, biased = sem("down_ok"), sem("down_used"), sem("y_ok"), sem("biased")
        pe_turn, dve_turn, pool_turn = sem("e_pe_turn"), sem("e_dve_turn"), sem("e_pool_turn")
        block = ctx.enter_context(nc.Block())
        PAIRS_E = SLOT_TILES // GT // 2

        @block.gpsimd
        def _(pool):
            def gather(i, s):
                nc.gpsimd.tensor_copy(from_row[:, s, :], who["read"][:, ds(i * (2 * GT) + s * GT, GT)]).then_inc(idx_ok, 1)
                nc.gpsimd.tensor_copy(to_row[:, s, :], who["write"][:, ds(i * (2 * GT) + s * GT, GT)]).then_inc(idx_ok, 1)
                pool.wait_ge(idx_ok, i * 4 + (2 * s + 2))
                pool.sem_inc(pool_turn, 1)
                for u in range(GT):
                    pool.indirect_dma_start(R[:, s, u, :], None, rows[:, :],
                                            bass.IndirectOffsetOnAxis(from_row[:, s, u:u + 1], 0)).then_inc(row_in[s], 16)

            def scatter(i, s):
                pool.wait_ge(y_ok, i * (2 * GT) + (s + 1) * GT)
                pool.sem_inc(pool_turn, 1)
                for u in range(GT):
                    pool.indirect_dma_start(out[:, :], bass.IndirectOffsetOnAxis(to_row[:, s, u:u + 1], 0),
                                            Y[:, s, u, :], None, bounds_check=NODES - 1,
                                            oob_is_err=False).then_inc(row_out[s], 16)

            def written(i, s):
                pool.wait_ge(row_out[s], i * (16 * GT) + 16 * GT)
                pool.sem_inc(pool_turn, 1)

            gather(0, 0)
            with pool.Fori(0, PAIRS_E - 1) as i:
                gather(i, 1)
                scatter(i, 0)
                written(i, 0)
                gather(i + 1, 0)
                scatter(i, 1)
                written(i, 1)
            gather(PAIRS_E - 1, 1)
            scatter(PAIRS_E - 1, 0)
            scatter(PAIRS_E - 1, 1)
            written(PAIRS_E - 1, 0)
            written(PAIRS_E - 1, 1)

        @block.vector
        def _(dve):
            def copy_turned(g):
                dve.wait_ge(tps_ok, g + 1)
                nc.vector.tensor_copy(xT[:, :, :], tps[:, :, :]).then_inc(xT_ok, 1)

            def finish(i, s):
                dve.wait_ge(row_in[s], i * (16 * GT) + 16 * GT)
                for u in range(GT):
                    n = i * (2 * GT) + (s * GT + u)
                    e = dve.value_load(expert[0:1, ds(n, 1)], min_val=0, max_val=EXPERTS - 1)
                    dve.wait_ge(down_ok, n + 1)
                    dve.sem_inc(dve_turn, 1)
                    y = Y[:, s, u, :]
                    nc.vector.tensor_tensor(y, down[:, u % 2, 0:D], bdr[:, ds(e * D, D)], ALU.add).then_inc(down_used, 1)
                    dve.wait_ge(down_used, n + 3)
                    dve.sem_inc(dve_turn, 1)
                    nc.vector.scalar_tensor_tensor(y, y, who["weight"][:, ds(n, 1)], R[:, s, u, 0:D],
                                                   ALU.mult, ALU.add).then_inc(y_ok, 1)

            copy_turned(0)
            with dve.Fori(0, PAIRS_E - 1) as i:
                for s in range(2):
                    copy_turned(i * 2 + (s + 1))
                    finish(i, s)
            copy_turned(2 * PAIRS_E - 1)
            finish(PAIRS_E - 1, 0)
            finish(PAIRS_E - 1, 1)

        @block.scalar
        def _(act):
            with act.Fori(0, 2 * PAIRS_E) as g:
                for j in range(KH):
                    act.wait_ge(up_ok, g * KH + (j + 1))
                    nc.scalar.activation(H[:, j, :], up[:, j % 2, :], ACT.Gelu, bias=b1c[:, j:j + 1]).then_inc(h_ok, 1)

        @block.tensor
        def _(pe):
            def turn(i, s):
                pe.wait_ge(row_in[s], i * (16 * GT) + 16 * GT)
                for t in range(GT):
                    for k in range(K1):
                        last = nc.tensor.transpose(tps[:, k, t * P:(t + 1) * P], R[:, s, t, D + k * P:D + (k + 1) * P], ident_f[:, :])
                last.then_inc(tps_ok, 1)

            def hidden(i, s):
                g = i * 2 + s
                pe.wait_ge(xT_ok, g + 1)
                for j in range(KH):
                    pe.wait_ge(h_ok, g * KH + (j - 1 + 2))
                    for k in range(K1):
                        last = nc.tensor.matmul(up[:, j % 2, :], w1[:, k, j * P:(j + 1) * P], xT[:, k, :],
                                                start=(k == 0), stop=(k == K1 - 1))
                    last.then_inc(up_ok, 1)

            def products(i, s):
                pe.wait_ge(h_ok, (i * 2 + s) * KH + (KH + 2))
                for u in range(GT):
                    n = i * (2 * GT) + (s * GT + u)
                    e = pe.value_load(expert[0:1, ds(n, 1)], min_val=0, max_val=EXPERTS - 1)
                    pe.wait_ge(down_used, n + 1)
                    pe.sem_inc(pe_turn, 1)
                    for j in range(KH):
                        last = nc.tensor.matmul(down[:, u % 2, 0:D], H[:, j, u * P:(u + 1) * P],
                                                wd[:, j, ds(e * D, D)], start=(j == 0), stop=(j == KH - 1))
                    last.then_inc(down_ok, 1)

            pe.sem_inc(h_ok, 2)
            pe.sem_inc(down_used, 2)
            turn(0, 0)
            with pe.Fori(0, PAIRS_E - 1) as i:
                hidden(i, 0)
                turn(i, 1)
                products(i, 0)
                hidden(i, 1)
                turn(i + 1, 0)
                products(i, 1)
            last_i = PAIRS_E - 1
            hidden(last_i, 0)
            turn(last_i, 1)
            products(last_i, 0)
            hidden(last_i, 1)
            products(last_i, 1)


def kernel(**inputs):
    import numpy as np
    import concourse.bacc as bacc
    from concourse.bass_utils import run_bass_kernel_spmd

    a = {n: np.asarray(v) for n, v in inputs.items()}
    rows = TILES * P
    edges = CHUNKS_PAD * P
    x = np.concatenate([a["x"], np.zeros((rows - NODES, D), np.float32)])
    src = np.concatenate([a["src"], np.zeros(edges - EDGES, np.int32)]).reshape(CHUNKS_PAD, P)
    dst = np.concatenate([a["dst"], np.full(edges - EDGES, NO_NODE, np.int32)]).reshape(CHUNKS_PAD, P)
    arrays = {
        "x": x,
        "src_cols": np.ascontiguousarray(src.T),
        "dst_cols": np.ascontiguousarray(dst.T),
        "dst_chunks": dst,
        "w01": np.ascontiguousarray(np.concatenate([a["L0_gnn_w0_w"], a["L0_gnn_w1_w"]]).T),
        "b01": np.concatenate([a["L0_gnn_w0_b"], a["L0_gnn_w1_b"]]),
        "W1": a["L0_ffn_W1"], "b1": a["L0_ffn_b1"], "Wg": a["L0_ffn_Wg"], "bg": a["L0_ffn_bg"],
        "Wd": a["L0_ffn_Wd"], "bd": a["L0_ffn_bd"],
    }
    nc = bacc.Bacc("TRN2", target_bir_lowering=False, num_devices=1)
    args = {n: nc.dram_tensor("in_" + n, v.shape, mybir.dt.from_np(v.dtype), kind="ExternalInput").ap()
            for n, v in arrays.items()}
    out = nc.dram_tensor("out", (NODES, D), mybir.dt.float32, kind="ExternalOutput").ap()
    build(nc, out=out, **args)
    r = run_bass_kernel_spmd(nc, [{"in_" + n: v for n, v in arrays.items()}], core_ids=[0])
    return r.results[0]["out"]
```
